# Optimizing a Trainium2 kernel written in Bass

```python
import numpy as np
import jax
import jax.numpy as jnp

def _softmax(x, axis=-1):
    return jax.nn.softmax(x, axis=axis)

def _gelu(x):
    return jax.nn.gelu(x, approximate=True)

def _silu(x):
    return jax.nn.silu(x)

def _sigmoid(x):
    return jax.nn.sigmoid(x)

def _layernorm(x, axis=-1, eps=1e-05):
    m = jnp.mean(x, axis=axis, keepdims=True)
    v = jnp.var(x, axis=axis, keepdims=True)
    return (x - m) / jnp.sqrt(v + eps)

def _scatter_add(tgt, idx, src, axis=0):
    return tgt.at[idx].add(src)

def _segment_sum(src, seg, n):
    return jax.ops.segment_sum(src, seg, n)
kernel_name = 'mk_gnn_resnorm_d4_gnn_r8_47f09b'

def setup_inputs(seed: int=0):
    np.random.seed(seed)
    _w = jnp.asarray

    def _rec_inputs():
        import jax
        import jax.numpy as jnp
        _gk = jax.random.key(seed)
        x = -0.0003713 + 1 * jax.random.normal(jax.random.fold_in(_gk, 1), (6250, 128), jnp.float32)
        src = jax.random.randint(jax.random.fold_in(_gk, 2), (100000,), 0, 6250, jnp.int32)
        dst = jnp.minimum((6250 * jax.random.uniform(jax.random.fold_in(_gk, 3), (100000,)) ** 2.0).astype(jnp.int32), 49999)
        _o = jnp.argsort(dst, stable=True)
        src = src[_o]
        dst = dst[_o]
        edge_attr_64 = 0.000167468 + 1.0002 * jax.random.normal(jax.random.fold_in(_gk, 12), (100000, 64), jnp.float32)
        edge_weight = jax.random.uniform(jax.random.fold_in(_gk, 14), (100000,), jnp.float32, 0.0, 1)
        return (x, src, dst, edge_attr_64, edge_weight)
    x, src, dst, edge_attr_64, edge_weight = _rec_inputs()

    def _L0_gnn_setup():
        import jax, jax.numpy as jnp
        import numpy as np
        N_NODES = 12500
        N_EDGES = 200000
        D = 128
        K = 2
        ALPHA = 0.5

        def _appnp(x, edge_index):
            n = x.shape[0]
            loops = jnp.arange(n, dtype=edge_index.dtype)
            src = jnp.concatenate([edge_index[0], loops])
            dst = jnp.concatenate([edge_index[1], loops])
            ew = jnp.ones_like(src, dtype=x.dtype)
            deg = jax.ops.segment_sum(ew, dst, num_segments=n)
            dinv = jnp.where(deg > 0, jax.lax.rsqrt(deg), 0.0)
            norm = dinv[src] * ew * dinv[dst]
            h = x
            for _ in range(K):
                msg = norm[:, None] * x[src]
                agg = jax.ops.segment_sum(msg, dst, num_segments=n)
                x = (1.0 - ALPHA) * agg + ALPHA * h
            return x
        key = jax.random.key(seed)
        ks = jax.random.split(key, 5)
        x = jax.random.normal(ks[0], (N_NODES, D), dtype=jnp.float32)
        edge_index = jax.random.randint(ks[1], (2, N_EDGES), 0, N_NODES, dtype=jnp.int32)
        s = 1.0 / np.sqrt(D)
        w1 = jax.random.uniform(ks[2], (D, D), jnp.float32, -s, s)
        b1 = jnp.zeros((D,), jnp.float32)
        w2 = jax.random.uniform(ks[3], (D, D), jnp.float32, -s, s)
        b2 = jnp.zeros((D,), jnp.float32)
        return {'x': x, 'edge_index': edge_index, 'w1': w1, 'b1': b1, 'w2': w2, 'b2': b2}
    _L0_gnn_all = _L0_gnn_setup()
    _L0_gnn_in = {k: v for k, v in _L0_gnn_all.items() if k in ('w1', 'b1', 'w2', 'b2')}
    del _L0_gnn_all

    def _L1_gnn_setup():
        import jax, jax.numpy as jnp
        import numpy as np
        from jax.ops import segment_sum
        N = 12500
        M = 2500
        E = 200000
        D_IN = 128
        D_OUT = 128
        key = jax.random.key(seed)
        k1, k2, k3, k4, k5, k6 = jax.random.split(key, 6)
        x = jax.random.normal(k1, (N, D_IN), dtype=jnp.float32)
        node_idx = jax.random.randint(k2, (E,), 0, N)
        he_idx = jax.random.randint(k3, (E,), 0, M)
        hyperedge_index = jnp.stack([node_idx, he_idx], axis=0)
        hyperedge_weight = jax.random.uniform(k4, (M,), dtype=jnp.float32)
        W = jax.random.normal(k5, (D_OUT, D_IN), dtype=jnp.float32) / np.sqrt(D_IN)
        b = jax.random.normal(k6, (D_OUT,), dtype=jnp.float32) * 0.01
        return {'x': x, 'hyperedge_index': hyperedge_index, 'hyperedge_weight': hyperedge_weight, 'W': W, 'b': b}
    _L1_gnn_all = _L1_gnn_setup()
    _L1_gnn_in = {k: v for k, v in _L1_gnn_all.items() if k in ('hyperedge_weight', 'W', 'b')}
    del _L1_gnn_all

    def _L2_gnn_setup():
        import jax, jax.numpy as jnp
        import numpy as np
        N_NODES = 12500
        D = 128
        N_EDGES = 200000
        N_LAYERS = 3

        def _spmm(vals, rows, cols, x, n):
            gathered = vals[:, None] * x[cols]
            return jax.ops.segment_sum(gathered, rows, num_segments=n)
        key = jax.random.key(seed)
        k1, k2, k3, k4 = jax.random.split(key, 4)
        emb = jax.random.normal(k1, (N_NODES, D), dtype=jnp.float32)
        vals = jax.random.uniform(k2, (N_EDGES,), dtype=jnp.float32)
        rows = jax.random.randint(k3, (N_EDGES,), 0, N_NODES, dtype=jnp.int64 if jax.config.jax_enable_x64 else jnp.int32)
        cols = jax.random.randint(k4, (N_EDGES,), 0, N_NODES, dtype=jnp.int64 if jax.config.jax_enable_x64 else jnp.int32)
        return {'emb': emb, 'vals': vals, 'rows': rows, 'cols': cols}
    _L2_gnn_all = _L2_gnn_setup()
    _L2_gnn_in = {k: v for k, v in _L2_gnn_all.items() if k in ()}
    del _L2_gnn_all

    def _L3_gnn_setup():
        import jax, jax.numpy as jnp
        import numpy as np
        N, E = (5000, 80000)
        IN_DIM, EDGE_DIM, HID = (128, 64, 128)
        key = jax.random.key(seed)
        ks = jax.random.split(key, 10)
        x = jax.random.normal(ks[0], (N, IN_DIM), dtype=jnp.float32)
        edge_index = jax.random.randint(ks[1], (2, E), 0, N, dtype=jnp.int64)
        edge_attr = jax.random.normal(ks[2], (E, EDGE_DIM), dtype=jnp.float32)
        Wh_w = jax.random.normal(ks[3], (EDGE_DIM, HID), dtype=jnp.float32) / np.sqrt(EDGE_DIM)
        Wh_b = jnp.zeros((HID,), dtype=jnp.float32)
        Wn_w = jax.random.normal(ks[4], (2 * IN_DIM, HID), dtype=jnp.float32) / np.sqrt(2 * IN_DIM)
        Wn_b = jnp.zeros((HID,), dtype=jnp.float32)
        w_e = jax.random.normal(ks[5], (HID, 1), dtype=jnp.float32) / np.sqrt(HID)
        ft_w = jax.random.normal(ks[6], (IN_DIM, IN_DIM), dtype=jnp.float32) / np.sqrt(IN_DIM)
        ft_b = jnp.zeros((IN_DIM,), dtype=jnp.float32)
        return {'x': x, 'edge_index': edge_index, 'edge_attr': edge_attr, 'Wh_w': Wh_w, 'Wh_b': Wh_b, 'Wn_w': Wn_w, 'Wn_b': Wn_b, 'w_e': w_e, 'ft_w': ft_w, 'ft_b': ft_b}
    _L3_gnn_all = _L3_gnn_setup()
    _L3_gnn_in = {k: v for k, v in _L3_gnn_all.items() if k in ('Wh_w', 'Wh_b', 'Wn_w', 'Wn_b', 'w_e', 'ft_w', 'ft_b')}
    del _L3_gnn_all
    return {'x': x, 'src': src, 'dst': dst, 'edge_attr_64': edge_attr_64, 'edge_weight': edge_weight, 'L0_gnn_w1': _L0_gnn_in['w1'], 'L0_gnn_b1': _L0_gnn_in['b1'], 'L0_gnn_w2': _L0_gnn_in['w2'], 'L0_gnn_b2': _L0_gnn_in['b2'], 'L1_gnn_hyperedge_weight': _L1_gnn_in['hyperedge_weight'], 'L1_gnn_W': _L1_gnn_in['W'], 'L1_gnn_b': _L1_gnn_in['b'], 'L3_gnn_Wh_w': _L3_gnn_in['Wh_w'], 'L3_gnn_Wh_b': _L3_gnn_in['Wh_b'], 'L3_gnn_Wn_w': _L3_gnn_in['Wn_w'], 'L3_gnn_Wn_b': _L3_gnn_in['Wn_b'], 'L3_gnn_w_e': _L3_gnn_in['w_e'], 'L3_gnn_ft_w': _L3_gnn_in['ft_w'], 'L3_gnn_ft_b': _L3_gnn_in['ft_b']}

def reference(x, src, dst, edge_attr_64, edge_weight, L0_gnn_w1, L0_gnn_b1, L0_gnn_w2, L0_gnn_b2, L1_gnn_hyperedge_weight, L1_gnn_W, L1_gnn_b, L3_gnn_Wh_w, L3_gnn_Wh_b, L3_gnn_Wn_w, L3_gnn_Wn_b, L3_gnn_w_e, L3_gnn_ft_w, L3_gnn_ft_b):
    import jax
    import jax.numpy as jnp

    def _L0_gnn_ref(x, edge_index, w1, b1, w2, b2):
        import jax, jax.numpy as jnp
        import numpy as np
        N_NODES = 12500
        N_EDGES = 200000
        D = 128
        K = 2
        ALPHA = 0.5

        def _appnp(x, edge_index):
            n = x.shape[0]
            loops = jnp.arange(n, dtype=edge_index.dtype)
            src = jnp.concatenate([edge_index[0], loops])
            dst = jnp.concatenate([edge_index[1], loops])
            ew = jnp.ones_like(src, dtype=x.dtype)
            deg = jax.ops.segment_sum(ew, dst, num_segments=n)
            dinv = jnp.where(deg > 0, jax.lax.rsqrt(deg), 0.0)
            norm = dinv[src] * ew * dinv[dst]
            h = x
            for _ in range(K):
                msg = norm[:, None] * x[src]
                agg = jax.ops.segment_sum(msg, dst, num_segments=n)
                x = (1.0 - ALPHA) * agg + ALPHA * h
            return x
        x = jax.nn.relu(_appnp(x, edge_index))
        x = x @ w1.T + b1
        x = x @ w2.T + b2
        return x

    def _L1_gnn_ref(x, hyperedge_index, hyperedge_weight, W, b):
        import jax, jax.numpy as jnp
        import numpy as np
        from jax.ops import segment_sum
        N = 12500
        M = 2500
        E = 200000
        D_IN = 128
        D_OUT = 128
        node_idx = hyperedge_index[0]
        he_idx = hyperedge_index[1]
        num_nodes = x.shape[0]
        num_he = hyperedge_weight.shape[0]
        d_e = segment_sum(jnp.ones_like(he_idx, dtype=x.dtype), he_idx, num_segments=num_he)
        d_e = jnp.clip(d_e, 1.0, None)
        d_v = segment_sum(hyperedge_weight[he_idx], node_idx, num_segments=num_nodes)
        d_v = jnp.clip(d_v, 1.0, None)
        d_v_inv_sqrt = d_v ** (-0.5)
        x_prime = x * d_v_inv_sqrt[:, None]
        he_feat = segment_sum(x_prime[node_idx], he_idx, num_segments=num_he)
        he_feat = he_feat * (hyperedge_weight / d_e)[:, None]
        out = segment_sum(he_feat[he_idx], node_idx, num_segments=num_nodes)
        out = out * d_v_inv_sqrt[:, None]
        return out @ W.T + b

    def _L2_gnn_ref(emb, vals, rows, cols):
        import jax, jax.numpy as jnp
        import numpy as np
        N_NODES = 12500
        D = 128
        N_EDGES = 200000
        N_LAYERS = 3

        def _spmm(vals, rows, cols, x, n):
            gathered = vals[:, None] * x[cols]
            return jax.ops.segment_sum(gathered, rows, num_segments=n)
        n = emb.shape[0]
        side = _spmm(vals, rows, cols, emb, n)
        light_out = (emb + N_LAYERS * side) / (N_LAYERS + 1)
        return light_out

    def _L3_gnn_ref(x, edge_index, edge_attr, Wh_w, Wh_b, Wn_w, Wn_b, w_e, ft_w, ft_b):
        import jax, jax.numpy as jnp
        import numpy as np
        N, E = (5000, 80000)
        IN_DIM, EDGE_DIM, HID = (128, 64, 128)
        src, dst = (edge_index[0], edge_index[1])
        node_feat = jnp.concatenate([x[src], x[dst]], axis=1)
        edge_h = edge_attr @ Wh_w + Wh_b
        node_h = node_feat @ Wn_w + Wn_b
        combined = jax.nn.relu(edge_h + node_h)
        scores = (combined @ w_e)[:, 0]
        alpha = jax.nn.softmax(scores, axis=0)
        local = jnp.zeros_like(x).at[src].add(-alpha[:, None] * x[dst])
        out = x + local
        out = out + out @ ft_w + ft_b
        return out
    edge_index = jnp.stack([src, dst])
    x = _layernorm(x + _L0_gnn_ref(x, edge_index, L0_gnn_w1, L0_gnn_b1, L0_gnn_w2, L0_gnn_b2), axis=-1)
    x = _layernorm(x + _L1_gnn_ref(x, edge_index, L1_gnn_hyperedge_weight, L1_gnn_W, L1_gnn_b), axis=-1)
    x = _layernorm(x + _L2_gnn_ref(x, edge_weight, src, dst), axis=-1)
    x = _layernorm(x + _L3_gnn_ref(x, edge_index, edge_attr_64, L3_gnn_Wh_w, L3_gnn_Wh_b, L3_gnn_Wn_w, L3_gnn_Wn_b, L3_gnn_w_e, L3_gnn_ft_w, L3_gnn_ft_b), axis=-1)
    return x

_drawn_inputs = setup_inputs


def setup_inputs(seed=0):
    import zlib

    import numpy as np

    out = dict(_drawn_inputs(seed))
    spreads = {'L0_gnn_b1': (0.0, 0.1),
     'L0_gnn_b2': (0.0, 0.1),
     'L3_gnn_Wh_b': (0.0, 0.8),
     'L3_gnn_Wn_b': (0.0, 0.8),
     'L3_gnn_ft_b': (0.0, 0.1)}
    factors = {'edge_attr_64': 57.452, 'L3_gnn_Wh_w': 53.029, 'L3_gnn_Wn_w': 53.741, 'L3_gnn_w_e': 53.625}
    for name, (base, spread) in spreads.items():
        noise = np.random.default_rng([zlib.crc32(name.encode()), seed]).standard_normal(out[name].shape)
        drawn = base * np.exp(spread * noise) if base else spread * noise
        out[name] = jnp.asarray(drawn.astype(out[name].dtype))
    for name, factor in factors.items():
        out[name] = (out[name] * factor).astype(out[name].dtype)
    return out
```

```python
import concourse.bass as bass
from concourse import mybir
from contextlib import ExitStack, contextmanager

FP32 = mybir.dt.float32
BF16 = mybir.dt.bfloat16
I32 = mybir.dt.int32
ALU = mybir.AluOpType
ACT = mybir.ActivationFunctionType
AX = mybir.AxisListType

P = 128
N, D = 6250, 128
E, DE = 100000, 64
M = 2500
NB = -(-N // P)
NP = NB * P
U = 16
HALF = U // 2
NI = -(-E // (P * U))
NT = NI * U
FULL = E // P
REST = E - FULL * P
CH = -(-NT // P)
WIN = P
PARK = NP
AW = NP + WIN
U3 = 32
BT = -(-(FULL + 1 + NB) // U3) * U3
ROW = DE + 4
MB = -(-M // P)
MH = M - (MB - 1) * P
NH = N - (NB - 1) * P
PAD = 30000.0
LOW = -3.0e38
Q3 = 8
assert NI == NB


class Names:
    pass


@contextmanager
def phase(nc, name, semaphores):
    made, S = [], {}
    for s in semaphores.split():
        base, _, n = s.partition("*")
        got = [nc.alloc_semaphore(f"{name}_{base}{k if n else ''}") for k in range(int(n or 1))]
        made += got
        S[base] = got if n else got[0]
    with nc.Block() as block:
        yield S, block
    nc.clear_and_free_semaphores(made)
    nc.all_engine_barrier()


def hold(eng, sem, value):
    eng.wait_ge(sem, value)
    eng.nop(nofuse=True)


def chain(eng, sem):
    count = [0]

    def step(ins):
        count[0] += 1
        ins.then_inc(sem, 1)
        eng.wait_ge(sem, count[0])
    return step


def window_starts(nc, engine, m, at, count):
    return nc.values_load_multi_w_load_instructions(m.startI[0:1, bass.ds(at, count)], engines=[engine], min_val=0, max_val=PARK,
                                                    skip_runtime_bounds_check_because="clamped to PARK")[1]


def node_view(dram, rows, width=D):
    return dram[0:rows, :].rearrange("(b p) d -> p b d", p=P)


def prepare(nc, m, a):
    nat = m.scratch
    w3 = CH * P
    natI = [nat[:, k * w3:(k + 1) * w3].bitcast(I32).rearrange("p (c e) -> p c e", e=P) for k in range(2)]
    natF = [nat[:, (2 + k) * w3:(3 + k) * w3].rearrange("p (c e) -> p c e", e=P) for k in range(3)]
    with phase(nc, "prepare", "filled loaded_edges loaded_x loaded_w iota dve hw_row consts nat transposed evacuated "
                              "diag replicated rep_used span_ready spanT span_read wT wT_used prefilled fill hist_ready "
                              "hist_used degree root scaled stored") as (S, block):
        FT = (CH - 1) * P
        LT = FULL - FT

        @block.sync
        def _(sp):
            sp.wait_ge(S["filled"], 5)
            for k, e in enumerate((a.src, a.dst)):
                sp.dma_start(natI[k][:, 0:CH - 1, :], e[0:FT * P].rearrange("(c p e) -> p c e", p=P, e=P)).then_inc(S["loaded_edges"], 16)
                sp.dma_start(natI[k][0:LT, CH - 1, :], e[FT * P:FULL * P].rearrange("(p e) -> p e", e=P)).then_inc(S["loaded_edges"], 16)
                sp.dma_start(natI[k][LT:LT + 1, CH - 1, 0:REST], e[FULL * P:E].rearrange("(p e) -> p e", p=1)).then_inc(S["loaded_edges"], 16)
            e = a.ew
            sp.dma_start(natF[2][:, 0:CH - 1, :], e[0:FT * P].rearrange("(c p e) -> p c e", p=P, e=P)).then_inc(S["loaded_edges"], 16)
            sp.dma_start(natF[2][0:LT, CH - 1, :], e[FT * P:FULL * P].rearrange("(p e) -> p e", e=P)).then_inc(S["loaded_edges"], 16)
            sp.dma_start(natF[2][LT:LT + 1, CH - 1, 0:REST], e[FULL * P:E].rearrange("(p e) -> p e", p=1)).then_inc(S["loaded_edges"], 16)
            sp.dma_start(m.x[:, 0:NB - 1, :], node_view(a.x, (NB - 1) * P)).then_inc(S["loaded_x"], 16)
            sp.dma_start(m.x[0:NH, NB - 1, :], a.x[(NB - 1) * P:N, :]).then_inc(S["loaded_x"], 16)
            for dst, src in ((m.w1, a.w1), (m.w2, a.w2), (m.W, a.W), (m.Wh, a.Wh), (m.ft, a.ft)):
                sp.dma_start(dst[:, :], src[:, :]).then_inc(S["loaded_w"], 16)
            sp.dma_start(m.Wn[:, 0, :], a.Wn[0:D, :]).then_inc(S["loaded_w"], 16)
            sp.dma_start(m.Wn[:, 1, :], a.Wn[D:2 * D, :]).then_inc(S["loaded_w"], 16)
            for k, b in enumerate((a.b2, a.b, a.bh, a.bn, a.ftb)):
                sp.dma_start(m.bias[:, k, :], b.rearrange("(o n) -> o n", o=1).broadcast_to([P, D])).then_inc(S["loaded_w"], 16)
            sp.dma_start(m.bias[:, 5, :], a.we.rearrange("n o -> o n").broadcast_to([P, D])).then_inc(S["loaded_w"], 16)
            sp.dma_start(m.b1[:, :], a.b1.rearrange("(n o) -> n o", o=1)).then_inc(S["loaded_w"], 16)
            sp.dma_start(m.hwn[:, 0:MB - 1], a.hw[0:(MB - 1) * P].rearrange("(b p) -> p b", p=P)).then_inc(S["loaded_w"], 16)
            sp.dma_start(m.hwn[0:MH, MB - 1:MB], a.hw[(MB - 1) * P:M].rearrange("(p o) -> p o", o=1)).then_inc(S["loaded_w"], 16)
            sp.wait_ge(S["fill"], 4)
            for i in range(BT // U):
                sp.dma_start(a.bucketed[i * U * P:(i + 1) * U * P, :].rearrange("(t p) d -> p t d", p=P),
                             m.erow[:, 0:U, :]).then_inc(S["prefilled"], 16)
            sp.wait_ge(S["scaled"], 1)
            sp.dma_start(node_view(a.table, NP), m.t[:, :, :]).then_inc(S["stored"], 16)
            sp.wait_ge(S["stored"], 16)
            sp.wait_ge(S["prefilled"], 16 * (BT // U))
            sp.wait_ge(S["loaded_w"], 16 * 16)

        @block.scalar
        def _(act):
            act.dma_start(m.side[:, 0:M], a.hw.rearrange("(o n) -> o n", o=1).broadcast_to([P, M])).then_inc(S["hw_row"], 16)
            act.wait_ge(S["hw_row"], 16)
            for k, dst in enumerate((m.w1T, m.w2T, m.WT)):
                act.wait_ge(S["wT"], k + 1)
                nc.scalar.copy(dst[:, :], m.ps[:, 4 + k, 0:P]).then_inc(S["wT_used"], 1)
            act.wait_ge(S["degree"], 1)
            nc.scalar.activation(m.dinv[:, :], m.deg[:, :], ACT.Sqrt).then_inc(S["root"], 1)

        @block.gpsimd
        def _(pool):
            nc.gpsimd.iota(m.iotaI[:, :], pattern=[[1, P]], base=0, channel_multiplier=0).then_inc(S["iota"], 1)
            nc.gpsimd.iota(m.pidxI[:, :], pattern=[[0, 1]], base=0, channel_multiplier=1).then_inc(S["iota"], 1)
            nc.gpsimd.iota(m.tI[:, :], pattern=[[1, BT]], base=0, channel_multiplier=0).then_inc(S["iota"], 1)
            nc.gpsimd.memset(m.erow[:, :, :], 0.0).then_inc(S["fill"], 1)
            pool.wait_ge(S["fill"], 1)
            nc.gpsimd.memset(m.erow[:, :, DE + 2:DE + 3], -1.0).then_inc(S["fill"], 1)
            nc.gpsimd.memset(m.agg[:, :], 0.0).then_inc(S["fill"], 1)
            nc.gpsimd.memset(m.hwe[:, :], 0.0).then_inc(S["fill"], 1)

        @block.vector
        def _(v):
            step = chain(v, S["dve"])
            V = nc.vector
            V.memset(natI[0][:, CH - 1, :], 0).then_inc(S["filled"], 1)
            V.memset(natI[1][:, CH - 1, :], int(PAD)).then_inc(S["filled"], 1)
            V.memset(natF[2][:, CH - 1, :], 0.0).then_inc(S["filled"], 1)
            V.memset(m.x[:, NB - 1, :], 0.0).then_inc(S["filled"], 1)
            V.memset(m.hwn[:, :], 0.0).then_inc(S["filled"], 1)
            step(V.memset(m.ones[:, :], 1.0))
            step(V.memset(m.zerob[:, :], 0.0))
            step(V.memset(m.zerof[:, :], 0.0))
            step(V.memset(m.lasthe[:, :], float(M - 1)))
            v.wait_ge(S["iota"], 3)
            step(V.tensor_copy(m.iota[:, :], m.iotaI[:, :]))
            step(V.tensor_copy(m.iotab[:, :], m.iotaI[:, :]))
            step(V.tensor_copy(m.pidx[:, :], m.pidxI[:, :]))
            step(V.tensor_scalar(m.ident[:, :], m.iota[:, :], m.pidx[:, 0:1], None, ALU.is_equal))
            step(V.tensor_copy(m.identb[:, :], m.ident[:, :]))
            V.tensor_scalar(m.tri[:, :], m.iota[:, :], m.pidx[:, 0:1], None, ALU.is_gt).then_inc(S["consts"], 1)
            v.wait_ge(S["loaded_edges"], 16 * 9)
            V.tensor_copy(natF[0], natI[0]).then_inc(S["nat"], 1)
            V.tensor_copy(natF[1], natI[1]).then_inc(S["nat"], 1)
            v.wait_ge(S["nat"], 2)
            step(V.tensor_reduce(m.tmin[:, :], natF[1], AX.X, ALU.min))
            real = natI[0].bitcast(FP32)
            step(V.scalar_tensor_tensor(real, natF[1], PAD, natF[1], ALU.is_lt, ALU.mult))
            step(V.tensor_reduce(m.tmax[:, :], real, AX.X, ALU.max))
            step(V.tensor_tensor(m.tmax[:, :], m.tmax[:, :], m.tmin[:, :], ALU.subtract))
            step(V.tensor_reduce(m.span[:, :], m.tmax[:, :], AX.X, ALU.max))
            V.tensor_scalar(m.tmin[:, :], m.tmin[:, :], float(PARK), None, ALU.min).then_inc(S["span_ready"], 1)
            v.wait_ge(S["span_ready"], 1)
            for n in range(3 * CH):
                k, c = n // CH, n % CH
                w = min(P, NT - c * P)
                v.wait_ge(S["transposed"], n + 1)
                V.tensor_copy((m.src, m.dst, m.ew)[k][:, c * P:c * P + w], m.ps[:, n % 4, 0:w]).then_inc(S["evacuated"], 1)
            for c in range(CH):
                w = min(P, NT - c * P)
                if c >= 2:
                    v.wait_ge(S["replicated"], c - 1)
                V.tensor_scalar(m.oh[:, c % 2, :], m.ident[:, :], m.tmin[:, c:c + 1], None, ALU.mult).then_inc(S["diag"], 1)
                v.wait_ge(S["replicated"], c + 1)
                V.tensor_copy(m.start[:, c * P:c * P + w], m.ps[:, c % 4, 0:w]).then_inc(S["rep_used"], 1)
            v.wait_ge(S["rep_used"], CH)
            v.wait_ge(S["spanT"], 1)
            V.tensor_reduce(m.small[0:1, 0:1], m.ps[0:1, 7, 0:P], AX.X, ALU.max).then_inc(S["span_read"], 1)
            v.wait_ge(S["span_read"], 1)
            step(V.tensor_copy(m.smallI[0:1, 0:1], m.small[0:1, 0:1]))
            step(V.tensor_scalar(m.smallI[0:1, 0:1], m.smallI[0:1, 0:1], 7, None, ALU.arith_shift_right))
            step(V.tensor_scalar(m.smallI[0:1, 0:1], m.smallI[0:1, 0:1], 1.0, None, ALU.add))
            row = m.tabs[0:1, 0:NT]
            step(V.tensor_copy(m.tF[:, :], m.tI[:, :]))
            step(V.tensor_scalar(row, m.start[0:1, 0:NT], float(M), None, ALU.is_lt))
            step(V.tensor_tensor(row, row, m.tF[0:1, 0:NT], ALU.mult))
            step(V.tensor_reduce(m.small[0:1, 1:2], row, AX.X, ALU.max))
            step(V.tensor_scalar(m.small[0:1, 1:2], m.small[0:1, 1:2], float(U), None, ALU.add))
            step(V.tensor_copy(m.smallI[0:1, 1:2], m.small[0:1, 1:2]))
            step(V.tensor_scalar(m.smallI[0:1, 1:2], m.smallI[0:1, 1:2], 4, None, ALU.arith_shift_right))
            for idx, hi, lo in ((m.dst, m.dhi, m.dlo), (m.src, m.shi, m.slo)):
                step(V.tensor_copy(m.wide, idx[:, 0:NT]))
                step(V.tensor_scalar(m.wide, m.wide, 7, None, ALU.arith_shift_right))
                step(V.tensor_copy(hi, m.wide))
                step(V.scalar_tensor_tensor(lo, hi, -float(P), idx[:, 0:NT], ALU.mult, ALU.add))
            step(V.memset(m.shi[:, FULL + 1:NT], 999.0))
            step(V.memset(m.shi[REST:64, FULL:FULL + 1], 999.0))
            step(V.memset(m.shi[64:P, FULL:FULL + 1], 999.0))
            v.wait_ge(S["hw_row"], 16)
            step(V.tensor_copy(m.side[:, M:AW], m.side[:, M - 1:M].to_broadcast([P, AW - M])))
            with v.Fori(0, NI) as i:
                for h in range(2):
                    v.wait_ge(S["hist_used"], i * 2 + h + 1)
                    cols = bass.ds(i * U + h * HALF, HALF)
                    V.tensor_tensor(m.ohhi[:, h * HALF:(h + 1) * HALF, :],
                                    m.dhi[:, cols].unsqueeze(2).to_broadcast([P, HALF, NB]),
                                    m.iota[:, 0:NB].unsqueeze(1).to_broadcast([P, HALF, NB]), ALU.is_equal).then_inc(S["hist_ready"], 1)
                    for k in range(HALF):
                        V.tensor_scalar(m.ohlo[:, h * HALF + k, :], m.iotab[:, :], m.dlo[:, bass.ds(i * U + h * HALF + k, 1)],
                                        None, ALU.is_equal).then_inc(S["hist_ready"], 1)
            v.wait_ge(S["hist_used"], 2 * NI + 3)
            V.tensor_scalar(m.deg[:, :], m.ps[:, 7, 0:NB], 1.0, None, ALU.add).then_inc(S["degree"], 1)
            v.wait_ge(S["root"], 1)
            step(V.reciprocal(m.dinv[:, :], m.dinv[:, :]))
            step(V.tensor_scalar(m.de[:, :], m.deg[:, :], -1.0, 1.0, ALU.add, ALU.max))
            v.wait_ge(S["loaded_x"], 32)
            V.tensor_tensor(m.t[:, :, :], m.x[:, :, :], m.dinv[:, :].unsqueeze(2).to_broadcast([P, NB, D]), ALU.mult).then_inc(S["scaled"], 1)

        @block.tensor
        def _(pe):
            T = nc.tensor
            pe.sem_inc(S["hist_used"], 2)
            pe.wait_ge(S["consts"], 1)
            pe.wait_ge(S["nat"], 2)
            for n in range(3 * CH):
                k, c = n // CH, n % CH
                w = min(P, NT - c * P)
                if n >= 4:
                    pe.wait_ge(S["evacuated"], n - 3)
                T.transpose(m.ps[:, n % 4, 0:w], natF[k][0:w, c, :], m.ident[0:w, 0:w]).then_inc(S["transposed"], 1)
            pe.wait_ge(S["loaded_w"], 16 * 16)
            for k, src in enumerate((m.w1, m.w2, m.W)):
                T.transpose(m.ps[:, 4 + k, 0:P], src[:, :], m.ident[:, :]).then_inc(S["wT"], 1)
            pe.wait_ge(S["span_ready"], 1)
            T.transpose(m.ps[0:1, 7, 0:P], m.span[:, 0:1], m.ident[:, :]).then_inc(S["spanT"], 1)
            for c in range(CH):
                w = min(P, NT - c * P)
                pe.wait_ge(S["diag"], c + 1)
                pe.wait_ge(S["evacuated"], 3 * CH)
                if c >= 4:
                    pe.wait_ge(S["rep_used"], c - 3)
                T.matmul(m.ps[:, c % 4, 0:w], m.ones[:, :], m.oh[:, c % 2, 0:w], start=True, stop=True).then_inc(S["replicated"], 1)
            pe.wait_ge(S["span_read"], 1)
            T.matmul(m.ps[:, 7, 0:NB], m.zerob[:, :], m.zerob[:, 0:NB], start=True, stop=False)
            with pe.Fori(0, NI) as i:
                for h in range(2):
                    for k in range(HALF):
                        pe.wait_ge(S["hist_ready"], i * 2 * (HALF + 1) + h * (HALF + 1) + k + 2)
                        last = T.matmul(m.ps[:, 7, 0:NB], m.ohlo[:, h * HALF + k, :], m.ohhi[:, h * HALF + k, :],
                                        start=False, stop=False)
                    last.then_inc(S["hist_used"], 1)
            T.matmul(m.ps[:, 7, 0:NB], m.zerob[:, :], m.zerob[:, 0:NB], start=False, stop=True).then_inc(S["hist_used"], 1)


def aggregate(nc, m, a, name, table, idx, dst_order, iters, weight=None, side=None, last_he=False, load_rows=False):
    off = m.off
    g = m.gather[:, 0:U * D].rearrange("p (t d) -> p t d", d=D)
    with phase(nc, name, f"landed*{U} idx_ready used onehot added round dve side picked rows*4 rows_read*4 meta reg") as (S, block):

        def rounds(eng):
            if not dst_order:
                return None
            n = eng.value_load(m.smallI[0:1, 0:1], min_val=1, max_val=NB + 1)
            return n

        def iterations(eng):
            if isinstance(iters, int):
                return iters
            return eng.value_load(iters, min_val=1, max_val=NI if dst_order else BT // U)

        def loops(eng, body, head=None):
            def bases(eng, i, n):
                body(eng.snap(i * U), eng.snap(n), eng.snap(n * U), i)

            R, I = rounds(eng), iterations(eng)
            if R is None:
                if head:
                    head(0)
                with eng.Fori(0, I) as i:
                    bases(eng, i, i)
            else:
                with eng.Fori(0, R) as r:
                    if head:
                        head(r)
                    with eng.Fori(0, I) as i:
                        bases(eng, i, r * I + i)

        if load_rows:
            @block.sync
            def _(sp):
                for q in range(4):
                    sp.sem_inc(S["rows_read"][q], 1)
                I = iterations(sp)
                with sp.Fori(0, I) as i:
                    for q in range(4):
                        hold(sp, S["rows_read"][q], i + 1)
                        sp.dma_start(m.erow[:, 4 * q:4 * q + 4, :],
                                     a.bucketed[bass.ds((i * U + 4 * q) * P, 4 * P), :].rearrange("(t p) d -> p t d", p=P)).then_inc(S["rows"][q], 16)

        @block.scalar
        def _(act):
            def body(t0, n, nt, i):
                for h in range(2):
                    cols = bass.ds(t0 + h * HALF, HALF)
                    if load_rows:
                        for q in (2 * h, 2 * h + 1):
                            act.wait_ge(S["rows"][q], nt + 16)
                            c4 = bass.ds(t0 + q * 4, 4)
                            r4 = m.erow[:, 4 * q:4 * q + 4, :]
                            nc.scalar.copy(m.ew[:, c4], r4[:, :, DE]).then_inc(S["meta"], 1)
                            nc.scalar.copy(m.dst[:, c4], r4[:, :, DE + 1]).then_inc(S["meta"], 1)
                            nc.scalar.copy(m.off[:, c4], r4[:, :, DE + 2]).then_inc(S["rows_read"][q], 1)
                        act.wait_ge(S["meta"], n * 8 + 4 * h + 4)
                    act.wait_ge(S["used"], nt + h * HALF + HALF)
                    if last_he:
                        nc.scalar.activation(m.clampf[:, h * HALF:(h + 1) * HALF], idx[:, cols], ACT.Relu,
                                             scale=-1.0, bias=m.lasthe[:, 0:1]).then_inc(S["reg"], 1)
                        act.wait_ge(S["reg"], n * 2 + h + 1)
                        nc.scalar.activation(m.idx[:, h * HALF:(h + 1) * HALF], m.clampf[:, h * HALF:(h + 1) * HALF],
                                             ACT.Identity, scale=-1.0, bias=m.lasthe[:, 0:1]).then_inc(S["idx_ready"], 1)
                    else:
                        nc.scalar.copy(m.idx[:, h * HALF:(h + 1) * HALF], idx[:, cols]).then_inc(S["idx_ready"], 1)
            loops(act, body)

        @block.gpsimd
        def _(pool):
            def body(t0, n, nt, i):
                for h in range(2):
                    hold(pool, S["idx_ready"], n * 2 + h + 1)
                    hold(pool, S["used"], nt + h * HALF + HALF)
                    for k in range(h * HALF, (h + 1) * HALF):
                        nc.gpsimd.indirect_dma_start(g[:, k, :], None, table,
                                                     bass.IndirectOffsetOnAxis(m.idx[:, k:k + 1], 0)).then_inc(S["landed"][k], 16)
            loops(pool, body)

        @block.tensor
        def _(pe):
            pe.sem_inc(S["used"], U)

            def body(t0, n, nt, i):
                for k in range(U):
                    pe.wait_ge(S["onehot"], nt + k + 1)
                    pe.wait_ge(S["landed"][k], nt + 16)
                    pe.wait_ge(S["added"], nt + k + 1)
                    nc.tensor.matmul(m.ps[:, k % 4, 0:P], g[:, k, :], m.oh[:, k % 8, :], start=True, stop=True).then_inc(S["used"], 1)
            loops(pe, body)

        @block.vector
        def _(v):
            V = nc.vector
            v.sem_inc(S["added"], 4)
            step = chain(v, S["dve"])
            if side:
                side.before(v, step, S)
            if dst_order:
                step(V.memset(m.shift[:, :], 0.0))

            def head(r):
                if not dst_order:
                    return
                V.tensor_scalar(off[:, 0:NT], m.start[:, 0:NT], m.shift[:, 0:1], float(PARK), ALU.add, ALU.min).then_inc(S["round"], 1)
                v.wait_ge(S["round"], r * 4 + 1)
                V.tensor_copy(m.startI[0:1, 0:NT], off[0:1, 0:NT]).then_inc(S["round"], 1)
                v.wait_ge(S["round"], r * 4 + 2)
                V.tensor_tensor(off[:, 0:NT], m.dst[:, 0:NT], off[:, 0:NT], ALU.subtract).then_inc(S["round"], 1)
                V.tensor_scalar(m.shift[:, :], m.shift[:, :], float(WIN), None, ALU.add).then_inc(S["round"], 1)
                hold(v, S["round"], r * 4 + 4)

            def body(t0, n, nt, i):
                start = window_starts(nc, mybir.EngineType.DVE, m, t0, U)
                if load_rows:
                    v.wait_ge(S["rows_read"][3], n + 2)
                    v.wait_ge(S["meta"], n * 8 + 8)
                    cols = bass.ds(t0, U)
                    V.tensor_tensor(off[:, cols], off[:, cols], m.start[:, cols], ALU.subtract).then_inc(S["round"], 1)
                    v.wait_ge(S["round"], n + 1)

                def onehots(q):
                    for k in range(4 * q, 4 * q + 4):
                        v.wait_ge(S["used"], nt + k + 9)
                        o = off[:, bass.ds(t0 + k, 1)]
                        if weight is None:
                            V.tensor_scalar(m.oh[:, k % 8, :], m.iota[:, :], o, None, ALU.is_equal).then_inc(S["onehot"], 1)
                        else:
                            V.tensor_scalar(m.oh[:, k % 8, :], m.iota[:, :], o, weight[:, bass.ds(t0 + k, 1)],
                                            ALU.is_equal, ALU.mult).then_inc(S["onehot"], 1)
                        if side:
                            side.tile(v, nt, k, start[k], o, S)

                def adds(q):
                    for k in range(4 * q, 4 * q + 4):
                        v.wait_ge(S["used"], nt + k + 1 + U)
                        v.wait_ge(S["added"], nt + k + 4)
                        w = m.agg[:, bass.ds(start[k], WIN)]
                        V.tensor_tensor(w, w, m.ps[:, k % 4, 0:P], ALU.add).then_inc(S["added"], 1)
                onehots(0)
                onehots(1)
                adds(0)
                onehots(2)
                adds(1)
                onehots(3)
                adds(2)
                adds(3)
                if side:
                    side.iteration(v, i, t0, n, nt, S)
            loops(v, body, head)


class HyperedgeWeights:

    def __init__(self, nc, m):
        self.nc, self.m = nc, m

    def before(self, v, step, S):
        v.sem_inc(S["picked"], 4)

    def tile(self, v, nt, k, start, o, S):
        m = self.m
        v.wait_ge(S["picked"], nt + k + 1)
        self.nc.vector.scalar_tensor_tensor(m.junk[:, k % 4, :], m.iota[:, :], o, m.side[:, bass.ds(start, WIN)],
                                            ALU.is_equal, ALU.mult, accum_out=m.picked[:, k:k + 1]).then_inc(S["picked"], 1)

    def iteration(self, v, i, t0, n, nt, S):
        m, V = self.m, self.nc.vector
        V.tensor_scalar(m.tabs[:, 0:NT], m.shi, m.iota[:, bass.ds(i, 1)], None, ALU.is_equal, ALU.add,
                        accum_out=m.cnt[:, bass.ds(i, 1)]).then_inc(S["side"], 1)
        v.wait_ge(S["side"], n * 2 + 1)
        v.wait_ge(S["picked"], nt + U + 4)
        cols = bass.ds(t0, U)
        V.tensor_tensor(m.hwe[:, cols], m.hwe[:, cols], m.picked[:, :], ALU.add).then_inc(S["side"], 1)
        v.wait_ge(S["side"], n * 2 + 2)


class BucketRanks:

    def __init__(self, nc, m):
        self.nc, self.m = nc, m

    def before(self, v, step, S):
        step(self.nc.vector.memset(self.m.rank[:, :], 0.0))

    def tile(self, v, nt, k, start, o, S):
        pass

    def iteration(self, v, i, t0, n, nt, S):
        m, V = self.m, self.nc.vector
        mask, cum = m.tabs[:, 0:NT], m.cum
        b = bass.ds(i, 1)
        V.tensor_scalar(mask, m.shi, m.iota[:, b], None, ALU.is_equal).then_inc(S["side"], 1)
        v.wait_ge(S["side"], n * 3 + 1)
        V.tensor_tensor_scan(cum, m.ones[:, 0:1].to_broadcast([P, NT]), mask, m.first[:, b], ALU.mult, ALU.add).then_inc(S["side"], 1)
        hold(v, S["side"], n * 3 + 2)
        V.copy_predicated(m.rank[:, 0:NT], mask.bitcast(I32), cum).then_inc(S["side"], 1)
        v.wait_ge(S["side"], n * 3 + 3)


def bucket_starts(nc, m):
    with phase(nc, "starts", "dve cnt_in_psum ends ends_in_psum") as (S, block):
        @block.vector
        def _(v):
            V, step = nc.vector, chain(v, S["dve"])
            v.wait_ge(S["cnt_in_psum"], 2)
            step(V.tensor_copy(m.bI[:, :], m.ps[:, 0, 0:NB]))
            step(V.tensor_scalar(m.bF[:, :], m.bI[:, :], float(P - 1), None, ALU.add))
            step(V.tensor_copy(m.bI[:, :], m.bF[:, :]))
            step(V.tensor_scalar(m.bI[:, :], m.bI[:, :], 7, None, ALU.arith_shift_right))
            step(V.tensor_copy(m.bF[:, :], m.bI[:, :]))
            step(V.tensor_tensor_scan(m.ends[:, :], m.ones[:, 0:1].to_broadcast([P, NB]), m.bF[:, :], 0.0, ALU.mult, ALU.add))
            step(V.tensor_tensor(m.bF[:, :], m.ends[:, :], m.bF[:, :], ALU.subtract))
            step(V.tensor_scalar(m.bF[:, :], m.bF[:, :], float(P), -1.0, ALU.mult, ALU.add))
            step(V.tensor_tensor(m.first[:, :], m.bF[:, :], m.ps[:, 1, 0:NB], ALU.add))
            for col, u, sh in ((2, U, 4), (3, U3, 5)):
                step(V.tensor_scalar(m.small[0:1, col:col + 1], m.ends[0:1, NB - 1:NB], float(u - 1), None, ALU.add))
                step(V.tensor_copy(m.smallI[0:1, col:col + 1], m.small[0:1, col:col + 1]))
                step(V.tensor_scalar(m.smallI[0:1, col:col + 1], m.smallI[0:1, col:col + 1], sh, None, ALU.arith_shift_right))
            V.tensor_copy(m.bF[:, :], m.ends[:, :]).then_inc(S["ends"], 1)
            v.wait_ge(S["ends_in_psum"], 1)
            step(V.tensor_copy(m.endp[0:NB, :], m.ps[0:NB, 2, 0:1]))

        @block.tensor
        def _(pe):
            nc.tensor.matmul(m.ps[:, 0, 0:NB], m.ones[:, :], m.cnt[:, :], start=True, stop=True).then_inc(S["cnt_in_psum"], 1)
            nc.tensor.matmul(m.ps[:, 1, 0:NB], m.tri[:, :], m.cnt[:, :], start=True, stop=True).then_inc(S["cnt_in_psum"], 1)
            pe.wait_ge(S["ends"], 1)
            nc.tensor.transpose(m.ps[0:NB, 2, 0:P], m.bF[:, :], m.ident[:, :]).then_inc(S["ends_in_psum"], 1)


def bucket_edges(nc, m, a):
    NQ, QT = 4, U // 4
    lo = m.gather[:, 0:U * P].rearrange("p (t n) -> p t n", n=P)
    hi = m.cumhi
    with phase(nc, "bucket", f"attr*{NQ} meta*{NQ} idx_ready scattered*{U} ready used_half weighed dve degree root started") as (S, block):
        def parts(i):
            return [(k, P if i * U + k < FULL else REST) for k in range(U) if i * U + k <= FULL]

        @block.sync
        def _(sp):
            def quarter(i, q):
                t0 = 4 * q
                sp.dma_start(m.erow[:, t0:t0 + QT, 0:DE],
                             a.attr[bass.ds((i * U + t0) * P, QT * P), :].rearrange("(t p) d -> p t d", p=P)).then_inc(S["attr"][q], 16)
            for q in range(NQ):
                quarter(0, q)
            with sp.Fori(1, NI - 1) as i:
                for q in range(NQ):
                    for k in range(QT * q, QT * q + QT):
                        hold(sp, S["scattered"][k], i * 16)
                    quarter(i, q)
            i = NI - 1
            for q in range(NQ):
                for k in range(QT * q, QT * q + QT):
                    hold(sp, S["scattered"][k], i * 16)
                for k, n in parts(i):
                    if k // QT == q:
                        e0 = (i * U + k) * P
                        sp.dma_start(m.erow[0:n, k, 0:DE], a.attr[e0:e0 + n, :]).then_inc(S["attr"][q], 16)
            for k, n in parts(i):
                sp.wait_ge(S["scattered"][k], NI * 16)

        @block.scalar
        def _(act):
            def body(i, tiles):
                for h in range(2):
                    for q in (2 * h, 2 * h + 1):
                        if not (isinstance(i, int) and i == 0):
                            for k in range(QT * q, QT * q + QT):
                                act.wait_ge(S["scattered"][k], i * 16)
                    nc.scalar.copy(m.idx[:, h * HALF:(h + 1) * HALF], m.rank[:, bass.ds(i * U + h * HALF, HALF)]).then_inc(S["idx_ready"], 1)
                    for q in (2 * h, 2 * h + 1):
                        w = min(QT, tiles - q * QT)
                        c4, r4 = bass.ds(i * U + q * QT, w), m.erow[:, QT * q:QT * q + w, :]
                        nc.scalar.copy(r4[:, :, DE], m.ew[:, c4]).then_inc(S["meta"][q], 1)
                        nc.scalar.copy(r4[:, :, DE + 1], m.dst[:, c4]).then_inc(S["meta"][q], 1)
                        nc.scalar.copy(r4[:, :, DE + 2], m.src[:, c4]).then_inc(S["meta"][q], 1)
            body(0, U)
            with act.Fori(1, NI - 1) as i:
                body(i, U)
            body(NI - 1, len(parts(NI - 1)))
            act.wait_ge(S["degree"], 1)
            nc.scalar.activation(m.dv[:, :], m.dv[:, :], ACT.Sqrt).then_inc(S["root"], 1)

        @block.gpsimd
        def _(pool):
            def scatter(k, n):
                nc.gpsimd.indirect_dma_start(a.bucketed, bass.IndirectOffsetOnAxis(m.idx[0:n, k:k + 1], 0), m.erow[0:n, k, :],
                                             None).then_inc(S["scattered"][k], 16)
            with pool.Fori(0, NI - 1) as i:
                for q in range(NQ):
                    hold(pool, S["idx_ready"], i * 2 + q // 2 + 1)
                    hold(pool, S["attr"][q], i * 16 + 16)
                    hold(pool, S["meta"][q], i * 3 + 3)
                    for k in range(QT * q, QT * q + QT):
                        scatter(k, P)
            i = NI - 1
            ps = parts(i)
            for q in range(NQ):
                mine = [x for x in ps if x[0] // QT == q]
                pool.wait_ge(S["idx_ready"], i * 2 + q // 2 + 1)
                pool.wait_ge(S["attr"][q], i * 16 + 16 * len(mine))
                pool.wait_ge(S["meta"][q], i * 3 + 3)
                for k, n in mine:
                    scatter(k, n)

        @block.vector
        def _(v):
            V, step = nc.vector, chain(v, S["dve"])
            v.sem_inc(S["used_half"], 2)
            with v.Fori(0, NI) as i:
                for h in range(2):
                    v.wait_ge(S["used_half"], i * 2 + h + 1)
                    cols = bass.ds(i * U + h * HALF, HALF)
                    hh = hi[:, h * HALF:(h + 1) * HALF, :]
                    V.tensor_tensor(hh, m.shi[:, cols].unsqueeze(2).to_broadcast([P, HALF, NB]),
                                    m.iota[:, 0:NB].unsqueeze(1).to_broadcast([P, HALF, NB]), ALU.is_equal).then_inc(S["weighed"], 1)
                    v.wait_ge(S["weighed"], i * 2 + h + 1)
                    V.tensor_tensor(hh, hh, m.hwe[:, cols].unsqueeze(2).to_broadcast([P, HALF, NB]), ALU.mult).then_inc(S["ready"], 1)
                    for k in range(HALF):
                        V.tensor_scalar(lo[:, h * HALF + k, :], m.iota[:, :], m.slo[:, bass.ds(i * U + h * HALF + k, 1)],
                                        None, ALU.is_equal).then_inc(S["ready"], 1)
            v.wait_ge(S["used_half"], 2 * NI + 3)
            V.tensor_scalar(m.dv[:, :], m.ps[:, 7, 0:NB], 1.0, None, ALU.max).then_inc(S["degree"], 1)
            v.wait_ge(S["root"], 1)
            step(V.reciprocal(m.dv[:, :], m.dv[:, :]))

        @block.tensor
        def _(pe):
            nc.tensor.matmul(m.ps[:, 7, 0:NB], m.zerof[:, :], m.zerof[:, 0:NB], start=True, stop=False).then_inc(S["started"], 1)
            with pe.Fori(0, NI) as i:
                for h in range(2):
                    for k in range(HALF):
                        pe.wait_ge(S["ready"], i * 2 * (HALF + 1) + h * (HALF + 1) + k + 2)
                        last = nc.tensor.matmul(m.ps[:, 7, 0:NB], lo[:, h * HALF + k, :], hi[:, h * HALF + k, :],
                                                start=False, stop=False)
                    last.then_inc(S["used_half"], 1)
            nc.tensor.matmul(m.ps[:, 7, 0:NB], m.zerof[:, :], m.zerof[:, 0:NB], start=False, stop=True).then_inc(S["used_half"], 1)


UB = 7
assert NB % UB == 0


def bcast(cols):
    return cols.unsqueeze(2).to_broadcast([P, cols.shape[1], D])


def agg_blocks(nc, m, name, blocks, ub, rhs, use, after, store, clear=True, extra=None):
    slots = m.gather[:, 0:ub * P].rearrange("p (j n) -> p j n", n=P)
    with phase(nc, name, "slot in_psum emptied dve done stored cleared") as (S, block):
        @block.scalar
        def _(act):
            with act.Fori(0, blocks // ub) as i:
                for j in range(ub):
                    act.wait_ge(S["in_psum"], i * ub + j + 1)
                    nc.scalar.copy(slots[:, j, :], m.agg[:, bass.ds((i * ub + j) * P, P)]).then_inc(S["slot"], 1)

        @block.tensor
        def _(pe):
            pe.sem_inc(S["in_psum"], ub)
            pe.sem_inc(S["emptied"], ub)
            with pe.Fori(0, blocks // ub) as i:
                for j in range(ub):
                    pe.wait_ge(S["slot"], i * ub + j + 1)
                    pe.wait_ge(S["emptied"], i * ub + j + 1)
                    if rhs is None:
                        nc.tensor.transpose(m.ps[:, j, 0:P], slots[:, j, :], m.ident[:, :]).then_inc(S["in_psum"], 1)
                    else:
                        nc.tensor.matmul(m.ps[:, j, 0:P], slots[:, j, :], rhs[:, :], start=True, stop=True).then_inc(S["in_psum"], 1)

        @block.vector
        def _(v):
            step = chain(v, S["dve"])
            with v.Fori(0, blocks // ub) as i:
                for j in range(ub):
                    v.wait_ge(S["in_psum"], i * ub + j + 1 + ub)
                    use(v, i * ub + j, m.ps[:, j, 0:P]).then_inc(S["emptied"], 1)
            v.wait_ge(S["emptied"], blocks + ub)
            after(v, step)
            v.sem_inc(S["done"], 1)

        @block.gpsimd
        def _(pool):
            if clear:
                pool.wait_ge(S["slot"], blocks)
                nc.gpsimd.memset(m.agg[:, :], 0.0).then_inc(S["cleared"], 1)

        if store:
            @block.sync
            def _(sp):
                sp.wait_ge(S["done"], 1)
                for k, (dst, src) in enumerate(store):
                    sp.dma_start(dst, src).then_inc(S["stored"], 16)
                sp.wait_ge(S["stored"], 16 * len(store))


def row_blocks(nc, m, name, rows, rhs, width, use, before, after, hidden=None):
    v3 = lambda k: m.gather[:, k * UB * P:(k + 1) * UB * P].rearrange("p (j n) -> p j n", n=P)
    row, col, hid = v3(0), v3(1), v3(2)
    with phase(nc, name, "rows_ok row turned col hid_psum hid out emptied_t emptied_h emptied dve") as (S, block):
        def free(eng, sem, i, j):
            eng.wait_ge(sem, i * UB + j + (2 if j == 0 else 1))

        @block.scalar
        def _(act):
            act.wait_ge(S["rows_ok"], 1)
            with act.Fori(0, NB // UB) as i:
                for j in range(UB):
                    act.wait_ge(S["turned"], i * UB + j + 1)
                    nc.scalar.copy(row[:, j, :], rows[:, bass.ds(i * UB + j, 1), :].rearrange("p o d -> p (o d)")).then_inc(S["row"], 1)
                for t in range(UB + 1):
                    if t < UB:
                        act.wait_ge(S["turned"], i * UB + t + 1 + UB)
                        act.wait_ge(S["out"], i * UB + t + 1)
                        nc.scalar.copy(col[:, t, :], m.ps[:, t % 2, 0:P]).then_inc(S["col"], 1)
                    if hidden and t >= 1:
                        act.wait_ge(S["hid_psum"], i * UB + t)
                        nc.scalar.activation(hid[:, t - 1, :], m.ps[:, 2 + (t - 1) % 2, 0:P], ACT.Identity,
                                             bias=hidden[1][:, 0:1]).then_inc(S["hid"], 1)

        @block.tensor
        def _(pe):
            pe.sem_inc(S["turned"], UB)
            pe.sem_inc(S["out"], UB)
            pe.sem_inc(S["emptied"], 2)
            with pe.Fori(0, NB // UB) as i:
                for t in range(UB + 2):
                    if t < UB:
                        pe.wait_ge(S["row"], i * UB + t + 1)
                        if t >= 2:
                            pe.wait_ge(S["col"], i * UB + t - 1)
                        nc.tensor.transpose(m.ps[:, t % 2, 0:P], row[:, t, :], m.ident[:, :]).then_inc(S["turned"], 1)
                    j = t - 1
                    if hidden and 0 <= j < UB:
                        pe.wait_ge(S["col"], i * UB + j + 1)
                        if j >= 2:
                            pe.wait_ge(S["hid"], i * UB + j - 1)
                        nc.tensor.matmul(m.ps[:, 2 + j % 2, 0:P], hidden[0][:, :], col[:, j, :], start=True, stop=True).then_inc(S["hid_psum"], 1)
                    j = t - 2
                    if j >= 0:
                        pe.wait_ge(S["hid"] if hidden else S["col"], i * UB + j + 1)
                        free(pe, S["emptied"], i, j)
                        nc.tensor.matmul(m.ps[:, 4 + j % 2, 0:width], (hid if hidden else col)[:, j, :], rhs, start=True, stop=True).then_inc(S["out"], 1)

        @block.vector
        def _(v):
            step = chain(v, S["dve"])
            before(v, step)
            v.sem_inc(S["rows_ok"], 1)
            with v.Fori(0, NB // UB) as i:
                for j in range(UB):
                    v.wait_ge(S["out"], i * UB + j + 1 + UB)
                    use(v, i * UB + j, m.ps[:, 4 + j % 2, 0:width]).then_inc(S["emptied"], 1)
            v.wait_ge(S["emptied"], NB + 2)
            after(v, step)


def layernorm(nc, m, name, store, before=None, after=None):
    with phase(nc, name, "dve stats mv kept var root normed done stored") as (S, block):
        @block.vector
        def _(v):
            V, step = nc.vector, chain(v, S["dve"])
            if before:
                before(v, step)
            blk = lambda b: m.x[:, bass.ds(b, 1), :].rearrange("p o d -> p (o d)")
            with v.Fori(0, NB // UB) as i:
                for j in range(UB):
                    V.bn_stats(m.stats[:, j, :], blk(i * UB + j)).then_inc(S["stats"], 1)
                hold(v, S["stats"], i * UB + UB)
                for j in range(UB):
                    V.bn_aggr(m.mv7[:, j, :], m.stats[:, j, :]).then_inc(S["mv"], 1)
                v.wait_ge(S["mv"], i * UB + UB)
                V.tensor_copy(m.mv[:, bass.ds(i * UB, UB), :], m.mv7[:, :, :]).then_inc(S["kept"], 1)
            v.wait_ge(S["kept"], NB // UB)
            V.tensor_scalar(m.rstd[:, :], m.mv[:, :, 1], 1e-5, None, ALU.add).then_inc(S["var"], 1)
            v.wait_ge(S["root"], 1)
            step(V.reciprocal(m.rstd[:, :], m.rstd[:, :]))
            with v.Fori(0, NB // UB) as i:
                for j in range(UB):
                    b = bass.ds(i * UB + j, 1)
                    V.tensor_scalar(blk(i * UB + j), blk(i * UB + j), m.mv[:, b, 0], m.rstd[:, b], ALU.subtract, ALU.mult).then_inc(S["normed"], 1)
            v.wait_ge(S["normed"], NB)
            if after:
                after(v, step)
            v.sem_inc(S["done"], 1)

        @block.scalar
        def _(act):
            act.wait_ge(S["var"], 1)
            nc.scalar.activation(m.rstd[:, :], m.rstd[:, :], ACT.Sqrt).then_inc(S["root"], 1)

        if store:
            @block.sync
            def _(sp):
                sp.wait_ge(S["done"], 1)
                for dst, src in store:
                    sp.dma_start(dst, src).then_inc(S["stored"], 16)
                sp.wait_ge(S["stored"], 16 * len(store))


def windows_of_buckets(nc, m):
    with phase(nc, "windows", "dve cmp in_psum") as (S, block):
        @block.vector
        def _(v):
            V, step = nc.vector, chain(v, S["dve"])
            V.tensor_scalar(m.tabs[0:NB, :], m.tF[0:NB, :], m.endp[0:NB, 0:1], None, ALU.is_ge).then_inc(S["cmp"], 1)
            v.wait_ge(S["in_psum"], 2)
            for k in range(2):
                step(V.tensor_scalar(m.start[:, k * (BT // 2):(k + 1) * (BT // 2)], m.ps[:, k, 0:BT // 2], float(P), None, ALU.mult))
            step(V.tensor_copy(m.startI[0:1, :], m.start[0:1, :]))
            step(V.memset(m.dst[:, :], 0.0))
            step(V.memset(m.off[:, :], -1.0))

        @block.tensor
        def _(pe):
            pe.wait_ge(S["cmp"], 1)
            for k in range(2):
                nc.tensor.matmul(m.ps[:, k, 0:BT // 2], m.ones[0:NB, :], m.tabs[0:NB, k * (BT // 2):(k + 1) * (BT // 2)],
                                 start=True, stop=True).then_inc(S["in_psum"], 1)


def attend(nc, m, a):
    NQ = U3 // Q3
    W2 = 2 * D
    g = m.gather[:, 0:U3 * W2].rearrange("p (t d) -> p t d", d=W2)
    with phase(nc, "attend", f"rows*{NQ} landed*{U3} idx_ready freed flags in_psum copied oneh "
                             "hidden summed scored max_in max_t max_new max_rep max_set expd rescaled z weights agg_in added "
                             "preset qd") as (S, block):
        @block.sync
        def _(sp):
            I = sp.value_load(m.smallI[0:1, 3:4], min_val=1, max_val=BT // U3)
            sp.sem_inc(S["in_psum"], 4 * Q3)
            with sp.Fori(0, I) as i:
                t0, s0, t2 = sp.snap(i * U3), sp.snap(i * NQ), sp.snap(i * (2 * U3))
                for q in range(NQ):
                    hold(sp, S["in_psum"], (t0 + q * Q3 + Q3) * 2)
                    h = q % 2
                    sp.dma_start(m.erow[:, h * Q3:(h + 1) * Q3, :],
                                 a.bucketed[bass.ds((t0 + q * Q3) * P, Q3 * P), :].rearrange("(t p) d -> p t d", p=P)).then_inc(S["rows"][q], 16)

        @block.gpsimd
        def _(pool):
            I = pool.value_load(m.smallI[0:1, 3:4], min_val=1, max_val=BT // U3)
            pool.sem_inc(S["freed"], U3)
            with pool.Fori(0, I) as i:
                t0, s0, t2 = pool.snap(i * U3), pool.snap(i * NQ), pool.snap(i * (2 * U3))
                for q in range(NQ):
                    hold(pool, S["idx_ready"], i * NQ + q + 1)
                    hold(pool, S["freed"], t0 + q * Q3 + Q3)
                    for k in range(q * Q3, q * Q3 + Q3):
                        nc.gpsimd.indirect_dma_start(g[:, k, :], None, a.table2,
                                                     bass.IndirectOffsetOnAxis(m.idx[:, k:k + 1], 0)).then_inc(S["landed"][k], 16)

        @block.scalar
        def _(act):
            I = act.value_load(m.smallI[0:1, 3:4], min_val=1, max_val=BT // U3)
            A = nc.scalar

            def cast(t, q):
                A.copy(m.idx[:, q * Q3:(q + 1) * Q3], m.dst[:, bass.ds(t + q * Q3, Q3)]).then_inc(S["idx_ready"], 1)

            for q in range(NQ):
                cast(0, q)
            with act.Fori(0, I) as i:
                t0, s0, t2 = act.snap(i * U3), act.snap(i * NQ), act.snap(i * (2 * U3))
                def copies(q):
                    for k in range(q * Q3, q * Q3 + Q3):
                        n = t0 + k
                        act.wait_ge(S["in_psum"], t2 + 2 * k + 2 + 4 * Q3)
                        act.wait_ge(S["hidden"], n + 1)
                        A.copy(m.eT[:, k % 4, :], m.ps[0:DE, k % 2, 0:P]).then_inc(S["copied"], 1)
                        A.copy(m.ohT[:, k % 4, :], m.psb[:, k % 2, 512:512 + P]).then_inc(S["copied"], 1)
                    act.wait_ge(S["summed"], t0 + q * Q3 + Q3 + 2)
                    cast(t0 + U3, q)

                def exps(q):
                    n = s0 + q
                    act.wait_ge(S["max_set"], n * 3 + 3)
                    A.activation(m.c[:, q:q + 1], m.dif[:, 0:1], ACT.Exp).then_inc(S["expd"], 1)
                    A.activation(m.p[:, q * Q3:(q + 1) * Q3], m.sc[:, q * Q3:(q + 1) * Q3], ACT.Exp, bias=m.negm[:, 0:1],
                                 accum_out=m.zq[:, 0:1]).then_inc(S["expd"], 1)
                copies(0)
                copies(1)
                exps(0)
                copies(2)
                exps(1)
                copies(3)
                exps(2)
                exps(3)

        @block.tensor
        def _(pe):
            I = pe.value_load(m.smallI[0:1, 3:4], min_val=1, max_val=BT // U3)
            T = nc.tensor
            pe.sem_inc(S["hidden"], 4)
            with pe.Fori(0, I) as i:
                t0, s0, t2 = pe.snap(i * U3), pe.snap(i * NQ), pe.snap(i * (2 * U3))
                def turn(q, k):
                    n = t0 + k
                    if k % Q3 == 0:
                        pe.wait_ge(S["rows"][q], i * 16 + 16)
                    pe.wait_ge(S["oneh"], n + 1)
                    hold(pe, S["copied"], t2 + 2 * k + 2)
                    T.transpose(m.ps[0:DE, k % 2, 0:P], m.erow[:, (q % 2) * Q3 + k % Q3, 0:DE], m.ident[:, :]).then_inc(S["in_psum"], 1)
                    T.transpose(m.psb[:, k % 2, 512:512 + P], m.ohb[:, k % 4, :], m.identb[:, :]).then_inc(S["in_psum"], 1)

                def hidden(q, k, start):
                    n = t0 + k
                    pe.wait_ge(S["copied"], t2 + 2 * k + 6)
                    pe.wait_ge(S["summed"], n + 1)
                    T.matmul(m.ps[:, 2 + k % 2, 0:P], m.eT[:, k % 4, :], m.Wh[:, :], start=True, stop=False)
                    T.matmul(m.ps[:, 2 + k % 2, 0:P], m.ohT[:, k % 4, :], m.side[:, bass.ds(start, P)], start=False, stop=True).then_inc(S["hidden"], 1)

                def scores(q):
                    start = window_starts(nc, mybir.EngineType.PE, m, t0 + q * Q3, Q3)
                    for t in range(Q3 + 1):
                        if t < Q3:
                            turn(q, q * Q3 + t)
                        if t >= 1:
                            hidden(q, q * Q3 + t - 1, start[t - 1])

                def turn_max(q):
                    n = s0 + q
                    pe.wait_ge(S["max_in"], n + 1)
                    T.transpose(m.ps[0:1, 6, 0:P], m.mx[:, 0:1], m.ident[:, :]).then_inc(S["max_t"], 1)

                def spread_max(q):
                    n = s0 + q
                    pe.wait_ge(S["max_new"], n + 1)
                    T.matmul(m.ps[:, 7, 0:1], m.ones[0:1, :], m.mnew[0:1, 0:1], start=True, stop=True).then_inc(S["max_rep"], 1)

                def sums(q):
                    for k in range(q * Q3, q * Q3 + Q3):
                        n = t0 + k
                        pe.wait_ge(S["weights"], n + 1)
                        pe.wait_ge(S["added"], n + 1 + U3 - 2)
                        T.matmul(m.ps[:, 4 + k % 2, 0:P], g[:, k, 0:D], m.oh[:, k % 4, :], start=True, stop=True).then_inc(S["freed"], 1)
                scores(0)
                turn_max(0)
                scores(1)
                spread_max(0)
                turn_max(1)
                sums(0)
                scores(2)
                spread_max(1)
                turn_max(2)
                sums(1)
                scores(3)
                spread_max(2)
                turn_max(3)
                sums(2)
                spread_max(3)
                sums(3)

        @block.vector
        def _(v):
            V, step = nc.vector, chain(v, S["preset"])
            step(V.memset(m.mrep[:, :], LOW))
            step(V.memset(m.hist[:, :], LOW))
            step(V.memset(m.z[:, :], 0.0))
            v.sem_inc(S["added"], U3)
            v.sem_inc(S["copied"], 4)
            v.sem_inc(S["summed"], 2)
            v.sem_inc(S["scored"], 4)
            I = v.value_load(m.smallI[0:1, 3:4], min_val=1, max_val=BT // U3)
            with v.Fori(0, I) as i:
                t0, s0, t2 = v.snap(i * U3), v.snap(i * NQ), v.snap(i * (2 * U3))
                start = None

                def scores(q):
                    for t in range(Q3 + 2):
                        if t < Q3:
                            k = q * Q3 + t
                            n = t0 + k
                            v.wait_ge(S["hidden"], n + 1)
                            V.tensor_scalar(m.ohb[:, k % 4, :], m.iotab[:, :], m.off[:, bass.ds(n, 1)], None, ALU.is_equal).then_inc(S["oneh"], 1)
                        if t >= 2:
                            k = q * Q3 + t - 2
                            n = t0 + k
                            v.wait_ge(S["hidden"], n + 1 + 4)
                            v.wait_ge(S["landed"][k], i * 16 + 16)
                            V.tensor_tensor(m.hid[:, k % 2, :], m.ps[:, 2 + k % 2, 0:P], g[:, k, D:W2], ALU.add).then_inc(S["summed"], 1)
                            v.wait_ge(S["summed"], n + 1 + 2)
                            v.wait_ge(S["scored"], n + 1)
                            V.scalar_tensor_tensor(m.junk[:, k % 4, :], m.hid[:, k % 2, :], 0.0, m.bias[:, 5, :], ALU.max, ALU.mult,
                                                   accum_out=m.sc[:, k:k + 1]).then_inc(S["scored"], 1)

                def local_max(q):
                    n = s0 + q
                    cols = slice(q * Q3, (q + 1) * Q3)
                    V.tensor_scalar(m.valid[:, 0:Q3], m.off[:, bass.ds(t0 + q * Q3, Q3)], 0.0, None, ALU.is_ge).then_inc(S["qd"], 1)
                    v.wait_ge(S["qd"], n * 4 + 1)
                    v.wait_ge(S["scored"], t0 + (q + 1) * Q3 + 4)
                    V.tensor_tensor(m.sc[:, cols], m.sc[:, cols], m.valid[:, 0:Q3], ALU.mult).then_inc(S["qd"], 1)
                    V.tensor_scalar(m.valid[:, Q3:2 * Q3], m.valid[:, 0:Q3], -1.0, -LOW, ALU.add, ALU.mult).then_inc(S["qd"], 1)
                    v.wait_ge(S["qd"], n * 4 + 3)
                    V.tensor_tensor(m.sc[:, cols], m.sc[:, cols], m.valid[:, Q3:2 * Q3], ALU.add).then_inc(S["qd"], 1)
                    v.wait_ge(S["qd"], n * 4 + 4)
                    V.tensor_reduce(m.mx[:, :], m.sc[:, cols], AX.X, ALU.max).then_inc(S["max_in"], 1)

                def new_max(q):
                    n = s0 + q
                    v.wait_ge(S["max_t"], n + 1)
                    V.tensor_reduce(m.mnew[0:1, 1:2], m.ps[0:1, 6, 0:P], AX.X, ALU.max).then_inc(S["flags"], 1)
                    v.wait_ge(S["flags"], n + 1)
                    V.tensor_tensor(m.mnew[0:1, 0:1], m.mnew[0:1, 1:2], m.mrep[0:1, 0:1], ALU.max).then_inc(S["max_new"], 1)

                def set_max(q):
                    n = s0 + q
                    v.wait_ge(S["max_rep"], n + 1)
                    V.tensor_tensor(m.dif[:, 0:1], m.mrep[:, 0:1], m.ps[:, 7, 0:1], ALU.subtract).then_inc(S["max_set"], 1)
                    v.wait_ge(S["max_set"], n * 3 + 1)
                    V.tensor_copy(m.mrep[:, 0:1], m.ps[:, 7, 0:1]).then_inc(S["max_set"], 1)
                    v.wait_ge(S["max_set"], n * 3 + 2)
                    V.tensor_copy(m.hist[:, bass.ds(n, 1)], m.mrep[:, 0:1]).then_inc(S["rescaled"], 1)
                    V.tensor_scalar(m.negm[:, 0:1], m.mrep[:, 0:1], -1.0, None, ALU.mult).then_inc(S["max_set"], 1)

                def sums(q):
                    n = s0 + q
                    v.wait_ge(S["expd"], n * 2 + 2)
                    V.tensor_scalar(m.z[:, 0:1], m.z[:, 0:1], m.c[:, q:q + 1], m.zq[:, 0:1], ALU.mult, ALU.add).then_inc(S["z"], 1)
                    v.wait_ge(S["z"], n + 1)
                    start = window_starts(nc, mybir.EngineType.DVE, m, t0 + q * Q3, Q3)
                    for t in range(Q3 + 2):
                        if t < Q3:
                            k = q * Q3 + t
                            tile = t0 + k
                            v.wait_ge(S["freed"], tile + 1 + U3 - 4)
                            V.tensor_scalar(m.oh[:, k % 4, :], m.iota[:, :], m.off[:, bass.ds(tile, 1)], m.p[:, k:k + 1],
                                            ALU.is_equal, ALU.mult).then_inc(S["weights"], 1)
                        if t >= 2:
                            k = q * Q3 + t - 2
                            tile = t0 + k
                            v.wait_ge(S["freed"], tile + 1 + U3)
                            v.wait_ge(S["added"], tile + U3)
                            w = m.agg[:, bass.ds(start[k % Q3], WIN)]
                            if k % Q3 == 0:
                                V.scalar_tensor_tensor(w, w, m.c[:, q:q + 1], m.ps[:, 4 + k % 2, 0:P], ALU.mult, ALU.add).then_inc(S["added"], 1)
                            else:
                                V.tensor_tensor(w, w, m.ps[:, 4 + k % 2, 0:P], ALU.add).then_inc(S["added"], 1)
                scores(0)
                local_max(0)
                scores(1)
                new_max(0)
                local_max(1)
                set_max(0)
                sums(0)
                scores(2)
                new_max(1)
                local_max(2)
                set_max(1)
                sums(1)
                scores(3)
                new_max(2)
                local_max(3)
                set_max(2)
                sums(2)
                new_max(3)
                set_max(3)
                sums(3)


def gnn_kernel(nc, x, src, dst, attr, ew, w1, b1, w2, b2, hw, W, b, Wh, bh, Wn, bn, we, ft, ftb, out):
    with ExitStack() as ctx, nc.allow_non_contiguous_dma(reason="2400 hyperedge weights"):
        def sb(name, shape, dt=FP32):
            return ctx.enter_context(nc.sbuf_tensor(name, shape, dt))

        a = Names()
        a.x, a.src, a.dst, a.attr, a.ew, a.hw = x, src, dst, attr, ew, hw
        a.w1, a.b1, a.w2, a.b2, a.W, a.b = w1, b1, w2, b2, W, b
        a.Wh, a.bh, a.Wn, a.bn, a.we, a.ft, a.ftb = Wh, bh, Wn, bn, we, ft, ftb
        a.table = nc.dram_tensor("node_table", (NP, D), FP32).ap()
        a.table2 = nc.dram_tensor("node_table_xq", (NP, 2 * D), FP32).ap()
        a.bucketed = nc.dram_tensor("bucketed_edges", (BT * P, ROW), FP32).ap()
        m = Names()
        m.x, m.t = sb("x_nodes", [P, NB, D]), sb("t_nodes", [P, NB, D])
        m.agg, m.side = sb("agg", [P, AW]), sb("side_rows", [P, AW])
        m.gather = sb("gathered", [P, U3 * 2 * D])
        up = m.gather[:, U * D:]
        m.scratch = up
        m.wide = up[:, 0:NT].bitcast(I32)
        m.dhi, m.dlo, m.cum = up[:, NT:2 * NT], up[:, 2 * NT:3 * NT], up[:, 3 * NT:4 * NT]
        m.shi, m.slo = up[:, 5 * CH * P:5 * CH * P + NT], up[:, 5 * CH * P + NT:5 * CH * P + 2 * NT]
        m.cumhi = up[:, 0:U * NB].rearrange("p (t b) -> p t b", b=NB)
        low = m.gather[:, 0:U * D].bitcast(BF16)
        m.ohlo = low[:, 0:U * P].rearrange("p (t n) -> p t n", n=P)
        m.ohhi = low[:, U * P:U * P + U * NB].rearrange("p (t n) -> p t n", n=NB)
        m.erow = sb("edge_rows", [P, U, ROW])
        BX = BT + U3
        m.src, m.dst, m.ew = sb("src_t", [P, NT]), sb("dst_t", [P, BX]), sb("ew_t", [P, BT])
        m.off, m.start, m.rank = sb("off_t", [P, BT]), sb("start_t", [P, BT]), sb("rank_t", [P, NT])
        m.hwe = sb("hwe_t", [P, NT])
        m.tabs = sb("tabs", [P, BT])
        m.tI = sb("tile_iota_i", [P, BT], I32)
        m.tF = m.tI[:, :].bitcast(FP32)
        m.startI = sb("start_i", [1, BT], I32)
        m.idx = sb("idx", [P, U3], I32)
        m.clampf = sb("clampf", [P, U])
        m.oh = sb("onehots", [P, 8, P])
        m.junk = sb("junk", [P, 4, P])
        m.picked = sb("picked", [P, U])
        m.iotaI, m.pidxI = sb("iota_i", [P, P], I32), sb("pidx_i", [P, 1], I32)
        m.iota, m.iotab, m.pidx = sb("iota", [P, P]), sb("iota_b", [P, P], BF16), sb("pidx", [P, 1])
        m.ident, m.identb, m.tri, m.ones = sb("ident", [P, P]), sb("ident_b", [P, P], BF16), sb("tri", [P, P]), sb("ones", [P, P])
        m.zerob, m.zerof = sb("zero_b", [P, P], BF16), sb("zero_f", [P, P])
        m.w1, m.w2, m.W = sb("w1", [P, D]), sb("w2", [P, D]), sb("W", [P, D])
        m.w1T, m.w2T, m.WT = sb("w1T", [P, D]), sb("w2T", [P, D]), sb("WT", [P, D])
        m.Wh, m.Wn, m.ft = sb("Wh", [DE, D]), sb("Wn", [P, 2, D]), sb("ft", [P, D])
        m.bias, m.b1 = sb("biases", [P, 6, D]), sb("b1", [P, 1])
        m.hwn = sb("hw_nodes", [P, MB])
        nb = lambda n, dt=FP32: sb(n, [P, NB], dt)
        m.dinv, m.deg, m.de, m.dv, m.cnt, m.first, m.ends, m.bF, m.rstd, m.fac = (
            nb(n) for n in ("dinv", "deg", "de", "dv", "cnt", "first", "ends", "bF", "rstd", "fac"))
        m.bI = nb("bI", I32)
        m.endp = sb("endp", [P, 1])
        m.tmin, m.tmax, m.span, m.shift = sb("tmin", [P, CH]), sb("tmax", [P, CH]), sb("span", [P, 1]), sb("shift", [P, 1])
        m.small, m.smallI, m.lasthe = sb("small", [P, 8]), sb("smallI", [1, 8], I32), sb("lasthe", [P, 1])
        m.mv7, m.stats, m.mv = sb("mv7", [P, UB, 2]), sb("stats", [P, UB, 6]), sb("mv", [P, NB, 2])
        m.eT, m.ohT, m.ohb = sb("eT", [DE, 4, P]), sb("ohT", [P, 4, P]), sb("ohb", [P, 4, P], BF16)
        m.hid = sb("hid", [P, 2, D])
        m.sc, m.p = sb("scores", [P, U3]), sb("probs", [P, U3])
        m.mrep, m.mx, m.mnew, m.dif, m.negm, m.zq, m.z = (sb(n, [P, 2]) for n in ("mrep", "mx2", "mnew", "dif", "negm", "zq", "z"))
        m.mx = m.mx[:, 0:1]
        m.c = sb("c", [P, U3 // Q3])
        m.valid = sb("valid", [P, 2 * Q3])
        m.hist = sb("max_hist", [P, BT // Q3])
        m.ps = ctx.enter_context(nc.psum_tensor("ps", [P, 8, 512], FP32))
        m.psb = m.ps[:, :, :].bitcast(BF16)
        V = nc.vector
        blk = lambda t, i: t[:, bass.ds(i, 1), :].rearrange("p o d -> p (o d)")
        prepare(nc, m, a)

        edges = dict(table=a.table, dst_order=True)
        aggregate(nc, m, a, "hop1", idx=m.src, iters=NI, side=HyperedgeWeights(nc, m), **edges)
        bucket_starts(nc, m)

        def add_self(v, i, ps):
            return V.tensor_tensor(blk(m.t, i), blk(m.t, i), ps, ALU.add)

        def hop1(v, step):
            t, x = m.t[:, :, :], m.x[:, :, :]
            step(V.tensor_tensor(t, t, bcast(m.dinv[:, :]), ALU.mult))
            step(V.tensor_tensor(t, t, x, ALU.add))
            step(V.tensor_scalar(m.bF[:, :], m.dinv[:, :], 0.5, None, ALU.mult))
            step(V.tensor_tensor(t, t, bcast(m.bF[:, :]), ALU.mult))
        agg_blocks(nc, m, "hop1_out", NB, UB, None, add_self, hop1, [(node_view(a.table, NP), m.t[:, :, :])])
        aggregate(nc, m, a, "hop2", idx=m.src, iters=NI, side=BucketRanks(nc, m), **edges)
        bucket_edges(nc, m, a)

        def hop2(v, step):
            t, x = m.t[:, :, :], m.x[:, :, :]
            step(V.tensor_tensor(t, t, bcast(m.dinv[:, :]), ALU.mult))
            step(V.tensor_tensor(t, t, x, ALU.add))
            step(V.tensor_scalar(t, t, 0.5, 0.0, ALU.mult, ALU.max))
        agg_blocks(nc, m, "hop2_out", NB, UB, None, add_self, hop2, None)
        row_blocks(nc, m, "mlp", m.t, m.w2T[:, :], D,
                   use=lambda v, i, ps: V.tensor_tensor(blk(m.x, i), blk(m.x, i), ps, ALU.add),
                   before=lambda v, step: None,
                   after=lambda v, step: step(V.tensor_tensor(m.x[:, :, :], m.x[:, :, :],
                                              m.bias[:, 0:1, :].to_broadcast([P, NB, D]), ALU.add)),
                   hidden=(m.w1T, m.b1))

        def scale_dv(v, step):
            step(V.tensor_tensor(m.t[:, :, :], m.x[:, :, :], bcast(m.dv[:, :]), ALU.mult))
        layernorm(nc, m, "norm0", [(node_view(a.table, NP), m.t[:, :, :])], after=scale_dv)
        aggregate(nc, m, a, "hyperedges", idx=m.src, iters=m.smallI[0:1, 1:2], **edges)

        def he_weight(v, step):
            n = (MB, 1)
            step(V.reciprocal(m.bF[:, 0:MB], m.de[:, 0:MB]))
            step(V.tensor_tensor(m.bF[:, 0:MB], m.bF[:, 0:MB], m.hwn[:, :], ALU.mult))
            step(V.tensor_tensor(m.t[:, 0:MB, :], m.t[:, 0:MB, :], bcast(m.bF[:, 0:MB]), ALU.mult))
        agg_blocks(nc, m, "he_out", MB, 5, None, lambda v, i, ps: V.tensor_copy(blk(m.t, i), ps), he_weight,
                   [(node_view(a.table, MB * P), m.t[:, 0:MB, :])])
        windows_of_buckets(nc, m)
        groups = m.smallI[0:1, 2:3]
        aggregate(nc, m, a, "members", table=a.table, idx=m.dst, dst_order=False, iters=groups, last_he=True, load_rows=True)

        def add_bias(v, step):
            step(V.tensor_tensor(m.x[:, :, :], m.x[:, :, :], m.bias[:, 1:2, :].to_broadcast([P, NB, D]), ALU.add))
        agg_blocks(nc, m, "members_out", NB, UB, m.WT,
                   lambda v, i, ps: V.scalar_tensor_tensor(blk(m.x, i), ps, m.dv[:, bass.ds(i, 1)], blk(m.x, i), ALU.mult, ALU.add),
                   add_bias, None)
        layernorm(nc, m, "norm1", [(node_view(a.table, NP), m.x[:, :, :])])

        aggregate(nc, m, a, "light", table=a.table, idx=m.dst, dst_order=False, iters=groups, weight=m.ew)
        agg_blocks(nc, m, "light_out", NB, UB, None,
                   lambda v, i, ps: V.scalar_tensor_tensor(blk(m.t, i), ps, 3.0, blk(m.x, i), ALU.mult, ALU.add),
                   lambda v, step: step(V.scalar_tensor_tensor(m.x[:, :, :].rearrange("p b d -> p (b d)"),
                                        m.t[:, :, :].rearrange("p b d -> p (b d)"), 0.25,
                                        m.x[:, :, :].rearrange("p b d -> p (b d)"), ALU.mult, ALU.add)), None)
        layernorm(nc, m, "norm2", [(node_view(a.table2[:, 0:D], NP), m.x[:, :, :])])

        def pq(v, i, ps):
            V.tensor_copy(m.side[:, bass.ds(i * P, P)], ps[:, 0:D])
            return V.tensor_copy(blk(m.t, i), ps[:, D:2 * D])

        def pq_bias(v, step):
            pn = m.side[:, 0:NP].rearrange("p (b d) -> p b d", d=D)
            for k in (2, 3):
                step(V.tensor_tensor(pn, pn, m.bias[:, k:k + 1, :].to_broadcast([P, NB, D]), ALU.add))
        row_blocks(nc, m, "pq", m.x, m.Wn[:, :, :].rearrange("p k d -> p (k d)"), 2 * D, pq, lambda v, step: None, pq_bias)
        store_q(nc, m, a)
        attend(nc, m, a)
        softmax_factors(nc, m)
        agg_blocks(nc, m, "attend_out", NB, UB, None,
                   lambda v, i, ps: V.scalar_tensor_tensor(blk(m.t, i), ps, m.fac[:, bass.ds(i, 1)], blk(m.x, i), ALU.mult, ALU.add),
                   lambda v, step: None, None, clear=False)

        def last(v, step):
            step(V.tensor_tensor(m.x[:, :, :], m.x[:, :, :], m.t[:, :, :], ALU.add))
            step(V.tensor_tensor(m.x[:, :, :], m.x[:, :, :], m.bias[:, 4:5, :].to_broadcast([P, NB, D]), ALU.add))
        row_blocks(nc, m, "ft", m.t, m.ft[:, :], D,
                   lambda v, i, ps: V.tensor_tensor(blk(m.x, i), blk(m.x, i), ps, ALU.add), lambda v, step: None, last)
        layernorm(nc, m, "norm3", [(node_view(out, (NB - 1) * P), m.x[:, 0:NB - 1, :]), (out[(NB - 1) * P:N, :], m.x[0:NH, NB - 1, :])])


def store_q(nc, m, a):
    with phase(nc, "store_q", "stored") as (S, block):
        @block.sync
        def _(sp):
            sp.dma_start(node_view(a.table2[:, D:2 * D], NP), m.t[:, :, :]).then_inc(S["stored"], 16)
            sp.wait_ge(S["stored"], 16)


def softmax_factors(nc, m):
    NQ = BT // Q3
    with phase(nc, "factors", "dve z_in_psum dif expd diag fac_psum") as (S, block):
        @block.vector
        def _(v):
            V, step = nc.vector, chain(v, S["dve"])
            mask = m.tabs[0:NB, 0:NQ]
            h = m.tabs[0:NB, NQ:2 * NQ]
            step(V.tensor_scalar(mask, m.tF[0:NB, 0:NQ], float(Q3), m.endp[0:NB, 0:1], ALU.mult, ALU.is_lt))
            step(V.tensor_tensor(h, m.hist[0:NB, :], mask, ALU.mult))
            step(V.tensor_scalar(mask, mask, -1.0, -LOW, ALU.add, ALU.mult))
            step(V.tensor_tensor(h, h, mask, ALU.add))
            step(V.tensor_reduce(m.small[0:NB, 5:6], h, AX.X, ALU.max))
            V.tensor_tensor(m.small[0:NB, 5:6], m.small[0:NB, 5:6], m.mrep[0:NB, 0:1], ALU.subtract).then_inc(S["dif"], 1)
            v.wait_ge(S["expd"], 1)
            V.tensor_scalar(m.oh[0:NB, 0, 0:NB], m.ident[0:NB, 0:NB], m.small[0:NB, 6:7], None, ALU.mult).then_inc(S["diag"], 1)
            v.wait_ge(S["z_in_psum"], 1)
            step(V.reciprocal(m.small[:, 7:8], m.ps[:, 0, 0:1]))
            v.wait_ge(S["fac_psum"], 1)
            step(V.tensor_scalar(m.fac[:, :], m.ps[:, 1, 0:NB], m.small[:, 7:8], -1.0, ALU.mult, ALU.mult))

        @block.scalar
        def _(act):
            act.wait_ge(S["dif"], 1)
            nc.scalar.activation(m.small[0:NB, 6:7], m.small[0:NB, 5:6], ACT.Exp).then_inc(S["expd"], 1)

        @block.tensor
        def _(pe):
            nc.tensor.matmul(m.ps[:, 0, 0:1], m.ones[:, :], m.z[:, 0:1], start=True, stop=True).then_inc(S["z_in_psum"], 1)
            pe.wait_ge(S["diag"], 1)
            nc.tensor.matmul(m.ps[:, 1, 0:NB], m.ones[0:NB, :], m.oh[0:NB, 0, 0:NB], start=True, stop=True).then_inc(S["fac_psum"], 1)


_INS = ["x", "src", "dst", "edge_attr_64", "edge_weight", "L0_gnn_w1", "L0_gnn_b1", "L0_gnn_w2", "L0_gnn_b2",
        "L1_gnn_hyperedge_weight", "L1_gnn_W", "L1_gnn_b", "L3_gnn_Wh_w", "L3_gnn_Wh_b", "L3_gnn_Wn_w", "L3_gnn_Wn_b",
        "L3_gnn_w_e", "L3_gnn_ft_w", "L3_gnn_ft_b"]


def kernel(**inputs):
    import numpy as _np
    import concourse.bacc as _bacc
    from concourse import mybir as _mybir
    from concourse.bass_utils import run_bass_kernel_spmd as _run

    nc = _bacc.Bacc("TRN2", target_bir_lowering=False, num_devices=1)
    nc.disable_value_cache = True
    arrays, args = {}, []
    for name in _INS:
        a = _np.ascontiguousarray(inputs[name])
        arrays[f"in_{name}_dram"] = a
        args.append(nc.dram_tensor(f"in_{name}_dram", a.shape, _mybir.dt.from_np(a.dtype), kind="ExternalInput").ap())
    args.append(nc.dram_tensor("out_0_dram", (N, D), _mybir.dt.float32, kind="ExternalOutput").ap())
    gnn_kernel(nc, *args)
    r = _run(nc, [arrays], core_ids=[0])
    return r.results[0]["out_0_dram"]
```

```python
import concourse.bass as bass
from concourse import mybir
from contextlib import ExitStack, contextmanager

FP32 = mybir.dt.float32
BF16 = mybir.dt.bfloat16
I32 = mybir.dt.int32
ALU = mybir.AluOpType
ACT = mybir.ActivationFunctionType
AX = mybir.AxisListType

P = 128
N, D = 6250, 128
E, DE = 100000, 64
M = 2500
NB = -(-N // P)
NP = NB * P
U = 16
HALF = U // 2
NI = -(-E // (P * U))
NT = NI * U
FULL = E // P
REST = E - FULL * P
CH = -(-NT // P)
WIN = P
PARK = NP
AW = NP + WIN
U3 = 32
BT = -(-(FULL + 1 + NB) // U3) * U3
ROW = DE + 4
MB = -(-M // P)
MH = M - (MB - 1) * P
NH = N - (NB - 1) * P
PAD = 30000.0
LOW = -3.0e38
Q3 = 8
G = 4
RG = U // G
assert Q3 == 2 * G and U3 // G % RG == 0
assert NI == NB


class Names:
    pass


@contextmanager
def phase(nc, name, semaphores):
    made, S = [], {}
    for s in semaphores.split():
        base, _, n = s.partition("*")
        got = [nc.alloc_semaphore(f"{name}_{base}{k if n else ''}") for k in range(int(n or 1))]
        made += got
        S[base] = got if n else got[0]
    with nc.Block() as block:
        yield S, block
    nc.clear_and_free_semaphores(made)
    nc.all_engine_barrier()


def hold(eng, sem, value):
    eng.wait_ge(sem, value)
    eng.nop(nofuse=True)


def chain(eng, sem):
    count = [0]

    def step(ins):
        count[0] += 1
        ins.then_inc(sem, 1)
        eng.wait_ge(sem, count[0])
    return step


def window_starts(nc, engine, m, at, count):
    return nc.values_load_multi_w_load_instructions(m.startI[0:1, bass.ds(at, count)], engines=[engine], min_val=0, max_val=PARK,
                                                    skip_runtime_bounds_check_because="clamped to PARK")[1]


def node_view(dram, rows, width=D):
    return dram[0:rows, :].rearrange("(b p) d -> p b d", p=P)


def prepare(nc, m, a):
    nat = m.scratch
    w3 = CH * P
    natI = [nat[:, k * w3:(k + 1) * w3].bitcast(I32).rearrange("p (c e) -> p c e", e=P) for k in range(2)]
    natF = [nat[:, (2 + k) * w3:(3 + k) * w3].rearrange("p (c e) -> p c e", e=P) for k in range(3)]
    with phase(nc, "prepare", "filled loaded_edges loaded_x loaded_w iota dve hw_row consts nat transposed evacuated "
                              "diag replicated rep_used span_ready spanT span_read wT wT_used prefilled fill hist_ready "
                              "hist_used degree root scaled stored") as (S, block):
        FT = (CH - 1) * P
        LT = FULL - FT

        @block.sync
        def _(sp):
            sp.wait_ge(S["filled"], 6)
            for k, e in enumerate((a.src, a.dst)):
                sp.dma_start(natI[k][:, 0:CH - 1, :], e[0:FT * P].rearrange("(c p e) -> p c e", p=P, e=P)).then_inc(S["loaded_edges"], 16)
                sp.dma_start(natI[k][0:LT, CH - 1, :], e[FT * P:FULL * P].rearrange("(p e) -> p e", e=P)).then_inc(S["loaded_edges"], 16)
                sp.dma_start(natI[k][LT:LT + 1, CH - 1, 0:REST], e[FULL * P:E].rearrange("(p e) -> p e", p=1)).then_inc(S["loaded_edges"], 16)
            e = a.ew
            sp.dma_start(natF[2][:, 0:CH - 1, :], e[0:FT * P].rearrange("(c p e) -> p c e", p=P, e=P)).then_inc(S["loaded_edges"], 16)
            sp.dma_start(natF[2][0:LT, CH - 1, :], e[FT * P:FULL * P].rearrange("(p e) -> p e", e=P)).then_inc(S["loaded_edges"], 16)
            sp.dma_start(natF[2][LT:LT + 1, CH - 1, 0:REST], e[FULL * P:E].rearrange("(p e) -> p e", p=1)).then_inc(S["loaded_edges"], 16)
            sp.dma_start(m.x[:, 0:NB - 1, :], node_view(a.x, (NB - 1) * P)).then_inc(S["loaded_x"], 16)
            sp.dma_start(m.x[0:NH, NB - 1, :], a.x[(NB - 1) * P:N, :]).then_inc(S["loaded_x"], 16)
            for dst, src in ((m.w1, a.w1), (m.w2, a.w2), (m.W, a.W), (m.ft, a.ft)):
                sp.dma_start(dst[:, :], src[:, :]).then_inc(S["loaded_w"], 16)
            for k in range(2):
                sp.dma_start(m.Wh[k * DE:(k + 1) * DE, k, :], a.Wh[:, :]).then_inc(S["loaded_w"], 16)
            sp.dma_start(m.Wn[:, 0, :], a.Wn[0:D, :]).then_inc(S["loaded_w"], 16)
            sp.dma_start(m.Wn[:, 1, :], a.Wn[D:2 * D, :]).then_inc(S["loaded_w"], 16)
            for k, b in enumerate((a.b2, a.b, a.bh, a.bn, a.ftb)):
                sp.dma_start(m.bias[:, k, :], b.rearrange("(o n) -> o n", o=1).broadcast_to([P, D])).then_inc(S["loaded_w"], 16)
            sp.dma_start(m.bias[:, 5, :], a.we.rearrange("n o -> o n").broadcast_to([P, D])).then_inc(S["loaded_w"], 16)
            sp.dma_start(m.b1[:, :], a.b1.rearrange("(n o) -> n o", o=1)).then_inc(S["loaded_w"], 16)
            sp.dma_start(m.hwn[:, 0:MB - 1], a.hw[0:(MB - 1) * P].rearrange("(b p) -> p b", p=P)).then_inc(S["loaded_w"], 16)
            sp.dma_start(m.hwn[0:MH, MB - 1:MB], a.hw[(MB - 1) * P:M].rearrange("(p o) -> p o", o=1)).then_inc(S["loaded_w"], 16)
            sp.wait_ge(S["fill"], 4)
            for i in range(BT // U):
                sp.dma_start(a.bucketed[i * U * P:(i + 1) * U * P, :].rearrange("(t p) d -> p t d", p=P),
                             m.erow[:, 0:U, :]).then_inc(S["prefilled"], 16)
            sp.wait_ge(S["scaled"], 1)
            sp.dma_start(node_view(a.table, NP), m.t[:, :, :]).then_inc(S["stored"], 16)
            sp.wait_ge(S["stored"], 16)
            sp.wait_ge(S["prefilled"], 16 * (BT // U))
            sp.wait_ge(S["loaded_w"], 16 * 17)

        @block.scalar
        def _(act):
            act.dma_start(m.side[:, 0:M], a.hw.rearrange("(o n) -> o n", o=1).broadcast_to([P, M])).then_inc(S["hw_row"], 16)
            act.wait_ge(S["hw_row"], 16)
            for k, dst in enumerate((m.w1T, m.w2T, m.WT)):
                act.wait_ge(S["wT"], k + 1)
                nc.scalar.copy(dst[:, :], m.ps[:, 4 + k, 0:P]).then_inc(S["wT_used"], 1)
            act.wait_ge(S["degree"], 1)
            nc.scalar.activation(m.dinv[:, :], m.deg[:, :], ACT.Sqrt).then_inc(S["root"], 1)

        @block.gpsimd
        def _(pool):
            nc.gpsimd.iota(m.iotaI[:, :], pattern=[[1, P]], base=0, channel_multiplier=0).then_inc(S["iota"], 1)
            nc.gpsimd.iota(m.pidxI[:, :], pattern=[[0, 1]], base=0, channel_multiplier=1).then_inc(S["iota"], 1)
            nc.gpsimd.iota(m.tI[:, :], pattern=[[1, BT]], base=0, channel_multiplier=0).then_inc(S["iota"], 1)
            nc.gpsimd.memset(m.erow[:, :, :], 0.0).then_inc(S["fill"], 1)
            pool.wait_ge(S["fill"], 1)
            nc.gpsimd.memset(m.erow[:, :, DE + 2:DE + 3], -1.0).then_inc(S["fill"], 1)
            nc.gpsimd.memset(m.agg[:, :], 0.0).then_inc(S["fill"], 1)
            nc.gpsimd.memset(m.hwe[:, :], 0.0).then_inc(S["fill"], 1)

        @block.vector
        def _(v):
            step = chain(v, S["dve"])
            V = nc.vector
            V.memset(natI[0][:, CH - 1, :], 0).then_inc(S["filled"], 1)
            V.memset(natI[1][:, CH - 1, :], int(PAD)).then_inc(S["filled"], 1)
            V.memset(natF[2][:, CH - 1, :], 0.0).then_inc(S["filled"], 1)
            V.memset(m.x[:, NB - 1, :], 0.0).then_inc(S["filled"], 1)
            V.memset(m.Wh[:, :, :], 0.0).then_inc(S["filled"], 1)
            V.memset(m.hwn[:, :], 0.0).then_inc(S["filled"], 1)
            step(V.memset(m.ones[:, :], 1.0))
            step(V.memset(m.zerob[:, :], 0.0))
            step(V.memset(m.zerof[:, :], 0.0))
            step(V.memset(m.lasthe[:, :], float(M - 1)))
            v.wait_ge(S["iota"], 3)
            step(V.tensor_copy(m.iota[:, :], m.iotaI[:, :]))
            step(V.tensor_copy(m.iotab[:, :], m.iotaI[:, :]))
            step(V.tensor_copy(m.pidx[:, :], m.pidxI[:, :]))
            step(V.tensor_scalar(m.ident[:, :], m.iota[:, :], m.pidx[:, 0:1], None, ALU.is_equal))
            step(V.tensor_copy(m.identb[:, :], m.ident[:, :]))
            V.tensor_scalar(m.tri[:, :], m.iota[:, :], m.pidx[:, 0:1], None, ALU.is_gt).then_inc(S["consts"], 1)
            v.wait_ge(S["loaded_edges"], 16 * 9)
            V.tensor_copy(natF[0], natI[0]).then_inc(S["nat"], 1)
            V.tensor_copy(natF[1], natI[1]).then_inc(S["nat"], 1)
            v.wait_ge(S["nat"], 2)
            step(V.tensor_reduce(m.tmin[:, :], natF[1], AX.X, ALU.min))
            real = natI[0].bitcast(FP32)
            step(V.scalar_tensor_tensor(real, natF[1], PAD, natF[1], ALU.is_lt, ALU.mult))
            step(V.tensor_reduce(m.tmax[:, :], real, AX.X, ALU.max))
            step(V.tensor_tensor(m.tmax[:, :], m.tmax[:, :], m.tmin[:, :], ALU.subtract))
            step(V.tensor_reduce(m.span[:, :], m.tmax[:, :], AX.X, ALU.max))
            V.tensor_scalar(m.tmin[:, :], m.tmin[:, :], float(PARK), None, ALU.min).then_inc(S["span_ready"], 1)
            v.wait_ge(S["span_ready"], 1)
            for n in range(3 * CH):
                k, c = n // CH, n % CH
                w = min(P, NT - c * P)
                v.wait_ge(S["transposed"], n + 1)
                V.tensor_copy((m.src, m.dst, m.ew)[k][:, c * P:c * P + w], m.ps[:, n % 4, 0:w]).then_inc(S["evacuated"], 1)
            for c in range(CH):
                w = min(P, NT - c * P)
                if c >= 2:
                    v.wait_ge(S["replicated"], c - 1)
                V.tensor_scalar(m.oh[:, c % 2, :], m.ident[:, :], m.tmin[:, c:c + 1], None, ALU.mult).then_inc(S["diag"], 1)
                v.wait_ge(S["replicated"], c + 1)
                V.tensor_copy(m.start[:, c * P:c * P + w], m.ps[:, c % 4, 0:w]).then_inc(S["rep_used"], 1)
            v.wait_ge(S["rep_used"], CH)
            v.wait_ge(S["spanT"], 1)
            V.tensor_reduce(m.small[0:1, 0:1], m.ps[0:1, 7, 0:P], AX.X, ALU.max).then_inc(S["span_read"], 1)
            v.wait_ge(S["span_read"], 1)
            step(V.tensor_copy(m.smallI[0:1, 0:1], m.small[0:1, 0:1]))
            step(V.tensor_scalar(m.smallI[0:1, 0:1], m.smallI[0:1, 0:1], 7, None, ALU.arith_shift_right))
            step(V.tensor_scalar(m.smallI[0:1, 0:1], m.smallI[0:1, 0:1], 1.0, None, ALU.add))
            row = m.tabs[0:1, 0:NT]
            step(V.tensor_copy(m.tF[:, :], m.tI[:, :]))
            step(V.tensor_scalar(row, m.start[0:1, 0:NT], float(M), None, ALU.is_lt))
            step(V.tensor_tensor(row, row, m.tF[0:1, 0:NT], ALU.mult))
            step(V.tensor_reduce(m.small[0:1, 1:2], row, AX.X, ALU.max))
            step(V.tensor_scalar(m.small[0:1, 1:2], m.small[0:1, 1:2], float(U), None, ALU.add))
            step(V.tensor_copy(m.smallI[0:1, 1:2], m.small[0:1, 1:2]))
            step(V.tensor_scalar(m.smallI[0:1, 1:2], m.smallI[0:1, 1:2], 4, None, ALU.arith_shift_right))
            for idx, hi, lo in ((m.dst, m.dhi, m.dlo), (m.src, m.shi, m.slo)):
                step(V.tensor_copy(m.wide, idx[:, 0:NT]))
                step(V.tensor_scalar(m.wide, m.wide, 7, None, ALU.arith_shift_right))
                step(V.tensor_copy(hi, m.wide))
                step(V.scalar_tensor_tensor(lo, hi, -float(P), idx[:, 0:NT], ALU.mult, ALU.add))
            step(V.memset(m.shi[:, FULL + 1:NT], 999.0))
            step(V.memset(m.shi[REST:64, FULL:FULL + 1], 999.0))
            step(V.memset(m.shi[64:P, FULL:FULL + 1], 999.0))
            v.wait_ge(S["hw_row"], 16)
            step(V.tensor_copy(m.side[:, M:AW], m.side[:, M - 1:M].to_broadcast([P, AW - M])))
            with v.Fori(0, NI) as i:
                for h in range(2):
                    v.wait_ge(S["hist_used"], i * 2 + h + 1)
                    cols = bass.ds(i * U + h * HALF, HALF)
                    V.tensor_tensor(m.ohhi[:, h * HALF:(h + 1) * HALF, :],
                                    m.dhi[:, cols].unsqueeze(2).to_broadcast([P, HALF, NB]),
                                    m.iota[:, 0:NB].unsqueeze(1).to_broadcast([P, HALF, NB]), ALU.is_equal).then_inc(S["hist_ready"], 1)
                    for k in range(HALF):
                        V.tensor_scalar(m.ohlo[:, h * HALF + k, :], m.iotab[:, :], m.dlo[:, bass.ds(i * U + h * HALF + k, 1)],
                                        None, ALU.is_equal).then_inc(S["hist_ready"], 1)
            v.wait_ge(S["hist_used"], 2 * NI + 3)
            V.tensor_scalar(m.deg[:, :], m.ps[:, 7, 0:NB], 1.0, None, ALU.add).then_inc(S["degree"], 1)
            v.wait_ge(S["root"], 1)
            step(V.reciprocal(m.dinv[:, :], m.dinv[:, :]))
            step(V.tensor_scalar(m.de[:, :], m.deg[:, :], -1.0, 1.0, ALU.add, ALU.max))
            v.wait_ge(S["loaded_x"], 32)
            V.tensor_tensor(m.t[:, :, :], m.x[:, :, :], m.dinv[:, :].unsqueeze(2).to_broadcast([P, NB, D]), ALU.mult).then_inc(S["scaled"], 1)

        @block.tensor
        def _(pe):
            T = nc.tensor
            pe.sem_inc(S["hist_used"], 2)
            pe.wait_ge(S["consts"], 1)
            pe.wait_ge(S["nat"], 2)
            for n in range(3 * CH):
                k, c = n // CH, n % CH
                w = min(P, NT - c * P)
                if n >= 4:
                    pe.wait_ge(S["evacuated"], n - 3)
                T.transpose(m.ps[:, n % 4, 0:w], natF[k][0:w, c, :], m.ident[0:w, 0:w]).then_inc(S["transposed"], 1)
            pe.wait_ge(S["loaded_w"], 16 * 17)
            for k, src in enumerate((m.w1, m.w2, m.W)):
                T.transpose(m.ps[:, 4 + k, 0:P], src[:, :], m.ident[:, :]).then_inc(S["wT"], 1)
            pe.wait_ge(S["span_ready"], 1)
            T.transpose(m.ps[0:1, 7, 0:P], m.span[:, 0:1], m.ident[:, :]).then_inc(S["spanT"], 1)
            for c in range(CH):
                w = min(P, NT - c * P)
                pe.wait_ge(S["diag"], c + 1)
                pe.wait_ge(S["evacuated"], 3 * CH)
                if c >= 4:
                    pe.wait_ge(S["rep_used"], c - 3)
                T.matmul(m.ps[:, c % 4, 0:w], m.ones[:, :], m.oh[:, c % 2, 0:w], start=True, stop=True).then_inc(S["replicated"], 1)
            pe.wait_ge(S["span_read"], 1)
            T.matmul(m.ps[:, 7, 0:NB], m.zerob[:, :], m.zerob[:, 0:NB], start=True, stop=False)
            with pe.Fori(0, NI) as i:
                for h in range(2):
                    for k in range(HALF):
                        pe.wait_ge(S["hist_ready"], i * 2 * (HALF + 1) + h * (HALF + 1) + k + 2)
                        last = T.matmul(m.ps[:, 7, 0:NB], m.ohlo[:, h * HALF + k, :], m.ohhi[:, h * HALF + k, :],
                                        start=False, stop=False)
                    last.then_inc(S["hist_used"], 1)
            T.matmul(m.ps[:, 7, 0:NB], m.zerob[:, :], m.zerob[:, 0:NB], start=False, stop=True).then_inc(S["hist_used"], 1)


def aggregate(nc, m, a, name, table, idx, dst_order, iters, weight=None, side=None, last_he=False, load_rows=False):
    off = m.off
    g = m.gather[:, 0:U * D].rearrange("p (t d) -> p t d", d=D)
    with phase(nc, name, f"landed*{U} idx_ready used onehot added round dve side picked rows*4 rows_read*4 meta reg window") as (S, block):

        def rounds(eng):
            if not dst_order:
                return None
            n = eng.value_load(m.smallI[0:1, 0:1], min_val=1, max_val=NB + 1)
            return n

        def iterations(eng):
            if isinstance(iters, int):
                return iters
            return eng.value_load(iters, min_val=1, max_val=NI if dst_order else BT // U)

        def loops(eng, body, head=None):
            def bases(eng, i, n):
                body(eng.snap(i * U), eng.snap(n), eng.snap(n * U), i)

            R, I = rounds(eng), iterations(eng)
            if R is None:
                if head:
                    head(0)
                with eng.Fori(0, I) as i:
                    bases(eng, i, i)
            else:
                with eng.Fori(0, R) as r:
                    if head:
                        head(r)
                    with eng.Fori(0, I) as i:
                        bases(eng, i, r * I + i)

        if load_rows:
            @block.sync
            def _(sp):
                for q in range(4):
                    sp.sem_inc(S["rows_read"][q], 1)
                I = iterations(sp)
                with sp.Fori(0, I) as i:
                    for q in range(4):
                        hold(sp, S["rows_read"][q], i + 1)
                        sp.dma_start(m.erow[:, 4 * q:4 * q + 4, :],
                                     a.bucketed[bass.ds((i * U + 4 * q) * P, 4 * P), :].rearrange("(t p) d -> p t d", p=P)).then_inc(S["rows"][q], 16)

        @block.scalar
        def _(act):
            def body(t0, n, nt, i):
                for q in range(4):
                    cols, here = bass.ds(t0 + 4 * q, 4), slice(4 * q, 4 * q + 4)
                    if load_rows:
                        act.wait_ge(S["rows"][q], nt + 16)
                        nc.scalar.copy(m.ew[:, cols], m.erow[:, here, DE]).then_inc(S["meta"], 1)
                        nc.scalar.copy(m.dst[:, cols], m.erow[:, here, DE + 1]).then_inc(S["meta"], 1)
                        nc.scalar.copy(m.off[:, cols], m.erow[:, here, DE + 2]).then_inc(S["rows_read"][q], 1)
                        act.wait_ge(S["meta"], n * 8 + 2 * q + 2)
                    act.wait_ge(S["used"], nt + 4 * q + 4)
                    if last_he:
                        nc.scalar.activation(m.clampf[:, here], idx[:, cols], ACT.Relu, scale=-1.0, bias=m.lasthe[:, 0:1]).then_inc(S["reg"], 1)
                        act.wait_ge(S["reg"], n * 4 + q + 1)
                        nc.scalar.activation(m.idx[:, here], m.clampf[:, here], ACT.Identity, scale=-1.0,
                                             bias=m.lasthe[:, 0:1]).then_inc(S["idx_ready"], 1)
                    else:
                        nc.scalar.copy(m.idx[:, here], idx[:, cols]).then_inc(S["idx_ready"], 1)
            loops(act, body)

        @block.gpsimd
        def _(pool):
            def body(t0, n, nt, i):
                for q in range(4):
                    hold(pool, S["idx_ready"], n * 4 + q + 1)
                    for k in range(4 * q, 4 * q + 4):
                        nc.gpsimd.indirect_dma_start(g[:, k, :], None, table,
                                                     bass.IndirectOffsetOnAxis(m.idx[:, k:k + 1], 0)).then_inc(S["landed"][k], 16)
            loops(pool, body)

        @block.tensor
        def _(pe):
            pe.sem_inc(S["used"], U)

            def body(t0, n, nt, i):
                for k in range(U):
                    pe.wait_ge(S["onehot"], nt + k + 1)
                    pe.wait_ge(S["landed"][k], nt + 16)
                    pe.wait_ge(S["added"], nt + k + 1)
                    nc.tensor.matmul(m.ps[:, k % 8, 0:P], g[:, k, :], m.oh[:, k % 8, :], start=True, stop=True).then_inc(S["used"], 1)
            loops(pe, body)

        @block.vector
        def _(v):
            V = nc.vector
            v.sem_inc(S["added"], 8)
            step = chain(v, S["dve"])
            if side:
                side.before(v, step, S)
            if dst_order:
                step(V.memset(m.shift[:, :], 0.0))

            def head(r):
                if not dst_order:
                    return
                V.tensor_scalar(off[:, 0:NT], m.start[:, 0:NT], m.shift[:, 0:1], float(PARK), ALU.add, ALU.min).then_inc(S["round"], 1)
                v.wait_ge(S["round"], r * 4 + 1)
                V.tensor_copy(m.startI[0:1, 0:NT], off[0:1, 0:NT]).then_inc(S["round"], 1)
                v.wait_ge(S["round"], r * 4 + 2)
                V.tensor_tensor(off[:, 0:NT], m.dst[:, 0:NT], off[:, 0:NT], ALU.subtract).then_inc(S["round"], 1)
                V.tensor_scalar(m.shift[:, :], m.shift[:, :], float(WIN), None, ALU.add).then_inc(S["round"], 1)
                hold(v, S["round"], r * 4 + 4)

            def body(t0, n, nt, i):
                start = window_starts(nc, mybir.EngineType.DVE, m, t0, U)
                if load_rows:
                    v.wait_ge(S["rows_read"][3], n + 2)
                    v.wait_ge(S["meta"], n * 8 + 8)
                    cols = bass.ds(t0, U)
                    V.tensor_tensor(off[:, cols], off[:, cols], m.start[:, cols], ALU.subtract).then_inc(S["round"], 1)
                    v.wait_ge(S["round"], n + 1)
                V.tensor_copy(m.now[:, 0:U], off[:, bass.ds(t0, U)]).then_inc(S["window"], 1)
                if weight is None:
                    v.wait_ge(S["window"], n + 1)
                else:
                    V.tensor_copy(m.wnow[:, 0:U], weight[:, bass.ds(t0, U)]).then_inc(S["window"], 1)
                    v.wait_ge(S["window"], n * 2 + 2)

                def onehots(q):
                    if side:
                        side.quarter(v, nt, q, S)
                    for k in range(4 * q, 4 * q + 4):
                        o = m.now[:, k:k + 1]
                        if weight is None:
                            V.tensor_scalar(m.oh[:, k % 8, :], m.iota[:, :], o, None, ALU.is_equal).then_inc(S["onehot"], 1)
                        else:
                            V.tensor_scalar(m.oh[:, k % 8, :], m.iota[:, :], o, m.wnow[:, k:k + 1],
                                            ALU.is_equal, ALU.mult).then_inc(S["onehot"], 1)
                        if side:
                            side.tile(v, nt, k, start[k], o, S)

                def adds(q):
                    v.wait_ge(S["used"], nt + 4 * q + 4 + U)
                    for k in range(4 * q, 4 * q + 4):
                        v.wait_ge(S["added"], nt + k + 8)
                        w = m.agg[:, bass.ds(start[k], WIN)]
                        V.tensor_tensor(w, w, m.ps[:, k % 8, 0:P], ALU.add).then_inc(S["added"], 1)
                onehots(0)
                onehots(1)
                adds(0)
                onehots(2)
                adds(1)
                onehots(3)
                adds(2)
                adds(3)
                if side:
                    side.iteration(v, i, t0, n, nt, S)
            loops(v, body, head)


class HyperedgeWeights:

    def __init__(self, nc, m):
        self.nc, self.m = nc, m

    def before(self, v, step, S):
        v.sem_inc(S["picked"], 4)

    def quarter(self, v, nt, q, S):
        v.wait_ge(S["picked"], nt + 4 * q + 4)

    def tile(self, v, nt, k, start, o, S):
        m = self.m
        self.nc.vector.scalar_tensor_tensor(m.junk[:, k % 4, :], m.iota[:, :], o, m.side[:, bass.ds(start, WIN)],
                                            ALU.is_equal, ALU.mult, accum_out=m.picked[:, k:k + 1]).then_inc(S["picked"], 1)

    def iteration(self, v, i, t0, n, nt, S):
        m, V = self.m, self.nc.vector
        V.tensor_scalar(m.tabs[:, 0:NT], m.shi, m.iota[:, bass.ds(i, 1)], None, ALU.is_equal, ALU.add,
                        accum_out=m.cnt[:, bass.ds(i, 1)]).then_inc(S["side"], 1)
        v.wait_ge(S["side"], n * 2 + 1)
        v.wait_ge(S["picked"], nt + U + 4)
        cols = bass.ds(t0, U)
        V.tensor_tensor(m.hwe[:, cols], m.hwe[:, cols], m.picked[:, :], ALU.add).then_inc(S["side"], 1)
        v.wait_ge(S["side"], n * 2 + 2)


class BucketRanks:

    def __init__(self, nc, m):
        self.nc, self.m = nc, m

    def before(self, v, step, S):
        step(self.nc.vector.memset(self.m.rank[:, :], 0.0))

    def quarter(self, v, nt, q, S):
        pass

    def tile(self, v, nt, k, start, o, S):
        pass

    def iteration(self, v, i, t0, n, nt, S):
        m, V = self.m, self.nc.vector
        mask, cum = m.tabs[:, 0:NT], m.cum
        b = bass.ds(i, 1)
        V.tensor_scalar(mask, m.shi, m.iota[:, b], None, ALU.is_equal).then_inc(S["side"], 1)
        v.wait_ge(S["side"], n * 3 + 1)
        V.tensor_tensor_scan(cum, m.ones[:, 0:1].to_broadcast([P, NT]), mask, m.first[:, b], ALU.mult, ALU.add).then_inc(S["side"], 1)
        hold(v, S["side"], n * 3 + 2)
        V.copy_predicated(m.rank[:, 0:NT], mask.bitcast(I32), cum).then_inc(S["side"], 1)
        v.wait_ge(S["side"], n * 3 + 3)


def bucket_starts(nc, m):
    with phase(nc, "starts", "dve cnt_in_psum ends ends_in_psum") as (S, block):
        @block.vector
        def _(v):
            V, step = nc.vector, chain(v, S["dve"])
            v.wait_ge(S["cnt_in_psum"], 2)
            step(V.tensor_copy(m.bI[:, :], m.ps[:, 0, 0:NB]))
            step(V.tensor_scalar(m.bF[:, :], m.bI[:, :], float(P - 1), None, ALU.add))
            step(V.tensor_copy(m.bI[:, :], m.bF[:, :]))
            step(V.tensor_scalar(m.bI[:, :], m.bI[:, :], 7, None, ALU.arith_shift_right))
            step(V.tensor_copy(m.bF[:, :], m.bI[:, :]))
            step(V.tensor_tensor_scan(m.ends[:, :], m.ones[:, 0:1].to_broadcast([P, NB]), m.bF[:, :], 0.0, ALU.mult, ALU.add))
            step(V.tensor_tensor(m.bF[:, :], m.ends[:, :], m.bF[:, :], ALU.subtract))
            step(V.tensor_scalar(m.bF[:, :], m.bF[:, :], float(P), -1.0, ALU.mult, ALU.add))
            step(V.tensor_tensor(m.first[:, :], m.bF[:, :], m.ps[:, 1, 0:NB], ALU.add))
            for col, u, sh in ((2, U, 4), (3, U3, 5)):
                step(V.tensor_scalar(m.small[0:1, col:col + 1], m.ends[0:1, NB - 1:NB], float(u - 1), None, ALU.add))
                step(V.tensor_copy(m.smallI[0:1, col:col + 1], m.small[0:1, col:col + 1]))
                step(V.tensor_scalar(m.smallI[0:1, col:col + 1], m.smallI[0:1, col:col + 1], sh, None, ALU.arith_shift_right))
            V.tensor_copy(m.bF[:, :], m.ends[:, :]).then_inc(S["ends"], 1)
            v.wait_ge(S["ends_in_psum"], 1)
            step(V.tensor_copy(m.endp[0:NB, :], m.ps[0:NB, 2, 0:1]))

        @block.tensor
        def _(pe):
            nc.tensor.matmul(m.ps[:, 0, 0:NB], m.ones[:, :], m.cnt[:, :], start=True, stop=True).then_inc(S["cnt_in_psum"], 1)
            nc.tensor.matmul(m.ps[:, 1, 0:NB], m.tri[:, :], m.cnt[:, :], start=True, stop=True).then_inc(S["cnt_in_psum"], 1)
            pe.wait_ge(S["ends"], 1)
            nc.tensor.transpose(m.ps[0:NB, 2, 0:P], m.bF[:, :], m.ident[:, :]).then_inc(S["ends_in_psum"], 1)


def bucket_edges(nc, m, a):
    NQ, QT = 4, U // 4
    lo = m.gather[:, 0:U * P].rearrange("p (t n) -> p t n", n=P)
    hi = m.cumhi
    with phase(nc, "bucket", f"attr*{NQ} meta*{NQ} idx_ready scattered*{U} ready used_half weighed dve degree root started") as (S, block):
        def parts(i):
            return [(k, P if i * U + k < FULL else REST) for k in range(U) if i * U + k <= FULL]

        @block.sync
        def _(sp):
            def quarter(i, q):
                t0 = 4 * q
                sp.dma_start(m.erow[:, t0:t0 + QT, 0:DE],
                             a.attr[bass.ds((i * U + t0) * P, QT * P), :].rearrange("(t p) d -> p t d", p=P)).then_inc(S["attr"][q], 16)
            for q in range(NQ):
                quarter(0, q)
            with sp.Fori(1, NI - 1) as i:
                for q in range(NQ):
                    for k in range(QT * q, QT * q + QT):
                        hold(sp, S["scattered"][k], i * 16)
                    quarter(i, q)
            i = NI - 1
            for q in range(NQ):
                for k in range(QT * q, QT * q + QT):
                    hold(sp, S["scattered"][k], i * 16)
                for k, n in parts(i):
                    if k // QT == q:
                        e0 = (i * U + k) * P
                        sp.dma_start(m.erow[0:n, k, 0:DE], a.attr[e0:e0 + n, :]).then_inc(S["attr"][q], 16)
            for k, n in parts(i):
                sp.wait_ge(S["scattered"][k], NI * 16)

        @block.scalar
        def _(act):
            def body(i, tiles):
                for h in range(2):
                    for q in (2 * h, 2 * h + 1):
                        if not (isinstance(i, int) and i == 0):
                            for k in range(QT * q, QT * q + QT):
                                act.wait_ge(S["scattered"][k], i * 16)
                    nc.scalar.copy(m.idx[:, h * HALF:(h + 1) * HALF], m.rank[:, bass.ds(i * U + h * HALF, HALF)]).then_inc(S["idx_ready"], 1)
                    for q in (2 * h, 2 * h + 1):
                        w = min(QT, tiles - q * QT)
                        c4, r4 = bass.ds(i * U + q * QT, w), m.erow[:, QT * q:QT * q + w, :]
                        nc.scalar.copy(r4[:, :, DE], m.ew[:, c4]).then_inc(S["meta"][q], 1)
                        nc.scalar.copy(r4[:, :, DE + 1], m.dst[:, c4]).then_inc(S["meta"][q], 1)
                        nc.scalar.copy(r4[:, :, DE + 2], m.src[:, c4]).then_inc(S["meta"][q], 1)
            body(0, U)
            with act.Fori(1, NI - 1) as i:
                body(i, U)
            body(NI - 1, len(parts(NI - 1)))
            act.wait_ge(S["degree"], 1)
            nc.scalar.activation(m.dv[:, :], m.dv[:, :], ACT.Sqrt).then_inc(S["root"], 1)

        @block.gpsimd
        def _(pool):
            def scatter(k, n):
                nc.gpsimd.indirect_dma_start(a.bucketed, bass.IndirectOffsetOnAxis(m.idx[0:n, k:k + 1], 0), m.erow[0:n, k, :],
                                             None).then_inc(S["scattered"][k], 16)
            with pool.Fori(0, NI - 1) as i:
                for q in range(NQ):
                    hold(pool, S["idx_ready"], i * 2 + q // 2 + 1)
                    hold(pool, S["attr"][q], i * 16 + 16)
                    hold(pool, S["meta"][q], i * 3 + 3)
                    for k in range(QT * q, QT * q + QT):
                        scatter(k, P)
            i = NI - 1
            ps = parts(i)
            for q in range(NQ):
                mine = [x for x in ps if x[0] // QT == q]
                pool.wait_ge(S["idx_ready"], i * 2 + q // 2 + 1)
                pool.wait_ge(S["attr"][q], i * 16 + 16 * len(mine))
                pool.wait_ge(S["meta"][q], i * 3 + 3)
                for k, n in mine:
                    scatter(k, n)

        @block.vector
        def _(v):
            V, step = nc.vector, chain(v, S["dve"])
            v.sem_inc(S["used_half"], 2)
            with v.Fori(0, NI) as i:
                for h in range(2):
                    v.wait_ge(S["used_half"], i * 2 + h + 1)
                    cols = bass.ds(i * U + h * HALF, HALF)
                    hh = hi[:, h * HALF:(h + 1) * HALF, :]
                    V.tensor_tensor(hh, m.shi[:, cols].unsqueeze(2).to_broadcast([P, HALF, NB]),
                                    m.iota[:, 0:NB].unsqueeze(1).to_broadcast([P, HALF, NB]), ALU.is_equal).then_inc(S["weighed"], 1)
                    v.wait_ge(S["weighed"], i * 2 + h + 1)
                    V.tensor_tensor(hh, hh, m.hwe[:, cols].unsqueeze(2).to_broadcast([P, HALF, NB]), ALU.mult).then_inc(S["ready"], 1)
                    for k in range(HALF):
                        V.tensor_scalar(lo[:, h * HALF + k, :], m.iota[:, :], m.slo[:, bass.ds(i * U + h * HALF + k, 1)],
                                        None, ALU.is_equal).then_inc(S["ready"], 1)
            v.wait_ge(S["used_half"], 2 * NI + 3)
            V.tensor_scalar(m.dv[:, :], m.ps[:, 7, 0:NB], 1.0, None, ALU.max).then_inc(S["degree"], 1)
            v.wait_ge(S["root"], 1)
            step(V.reciprocal(m.dv[:, :], m.dv[:, :]))

        @block.tensor
        def _(pe):
            nc.tensor.matmul(m.ps[:, 7, 0:NB], m.zerof[:, :], m.zerof[:, 0:NB], start=True, stop=False).then_inc(S["started"], 1)
            with pe.Fori(0, NI) as i:
                for h in range(2):
                    for k in range(HALF):
                        pe.wait_ge(S["ready"], i * 2 * (HALF + 1) + h * (HALF + 1) + k + 2)
                        last = nc.tensor.matmul(m.ps[:, 7, 0:NB], lo[:, h * HALF + k, :], hi[:, h * HALF + k, :],
                                                start=False, stop=False)
                    last.then_inc(S["used_half"], 1)
            nc.tensor.matmul(m.ps[:, 7, 0:NB], m.zerof[:, :], m.zerof[:, 0:NB], start=False, stop=True).then_inc(S["used_half"], 1)


UB = 7
assert NB % UB == 0


def bcast(cols):
    return cols.unsqueeze(2).to_broadcast([P, cols.shape[1], D])


def agg_blocks(nc, m, name, blocks, ub, rhs, use, after, store, clear=True, extra=None):
    slots = m.gather[:, 0:ub * P].rearrange("p (j n) -> p j n", n=P)
    with phase(nc, name, "slot in_psum emptied dve done stored cleared") as (S, block):
        @block.scalar
        def _(act):
            with act.Fori(0, blocks // ub) as i:
                for j in range(ub):
                    act.wait_ge(S["in_psum"], i * ub + j + 1)
                    nc.scalar.copy(slots[:, j, :], m.agg[:, bass.ds((i * ub + j) * P, P)]).then_inc(S["slot"], 1)

        @block.tensor
        def _(pe):
            pe.sem_inc(S["in_psum"], ub)
            pe.sem_inc(S["emptied"], ub)
            with pe.Fori(0, blocks // ub) as i:
                for j in range(ub):
                    pe.wait_ge(S["slot"], i * ub + j + 1)
                    pe.wait_ge(S["emptied"], i * ub + j + 1)
                    if rhs is None:
                        nc.tensor.transpose(m.ps[:, j, 0:P], slots[:, j, :], m.ident[:, :]).then_inc(S["in_psum"], 1)
                    else:
                        nc.tensor.matmul(m.ps[:, j, 0:P], slots[:, j, :], rhs[:, :], start=True, stop=True).then_inc(S["in_psum"], 1)

        @block.vector
        def _(v):
            step = chain(v, S["dve"])
            with v.Fori(0, blocks // ub) as i:
                for j in range(ub):
                    v.wait_ge(S["in_psum"], i * ub + j + 1 + ub)
                    use(v, i * ub + j, m.ps[:, j, 0:P]).then_inc(S["emptied"], 1)
            v.wait_ge(S["emptied"], blocks + ub)
            after(v, step)
            v.sem_inc(S["done"], 1)

        @block.gpsimd
        def _(pool):
            if clear:
                pool.wait_ge(S["slot"], blocks)
                nc.gpsimd.memset(m.agg[:, :], 0.0).then_inc(S["cleared"], 1)

        if store:
            @block.sync
            def _(sp):
                sp.wait_ge(S["done"], 1)
                for k, (dst, src) in enumerate(store):
                    sp.dma_start(dst, src).then_inc(S["stored"], 16)
                sp.wait_ge(S["stored"], 16 * len(store))


def row_blocks(nc, m, name, rows, rhs, width, use, before, after, hidden=None):
    v3 = lambda k: m.gather[:, k * UB * P:(k + 1) * UB * P].rearrange("p (j n) -> p j n", n=P)
    row, col, hid = v3(0), v3(1), v3(2)
    with phase(nc, name, "rows_ok row turned col hid_psum hid out emptied_t emptied_h emptied dve") as (S, block):
        def free(eng, sem, i, j):
            eng.wait_ge(sem, i * UB + j + (2 if j == 0 else 1))

        @block.scalar
        def _(act):
            act.wait_ge(S["rows_ok"], 1)
            with act.Fori(0, NB // UB) as i:
                for j in range(UB):
                    act.wait_ge(S["turned"], i * UB + j + 1)
                    nc.scalar.copy(row[:, j, :], rows[:, bass.ds(i * UB + j, 1), :].rearrange("p o d -> p (o d)")).then_inc(S["row"], 1)
                for t in range(UB + 1):
                    if t < UB:
                        act.wait_ge(S["turned"], i * UB + t + 1 + UB)
                        act.wait_ge(S["out"], i * UB + t + 1)
                        nc.scalar.copy(col[:, t, :], m.ps[:, t % 2, 0:P]).then_inc(S["col"], 1)
                    if hidden and t >= 1:
                        act.wait_ge(S["hid_psum"], i * UB + t)
                        nc.scalar.activation(hid[:, t - 1, :], m.ps[:, 2 + (t - 1) % 2, 0:P], ACT.Identity,
                                             bias=hidden[1][:, 0:1]).then_inc(S["hid"], 1)

        @block.tensor
        def _(pe):
            pe.sem_inc(S["turned"], UB)
            pe.sem_inc(S["out"], UB)
            pe.sem_inc(S["emptied"], 2)
            with pe.Fori(0, NB // UB) as i:
                for t in range(UB + 2):
                    if t < UB:
                        pe.wait_ge(S["row"], i * UB + t + 1)
                        if t >= 2:
                            pe.wait_ge(S["col"], i * UB + t - 1)
                        nc.tensor.transpose(m.ps[:, t % 2, 0:P], row[:, t, :], m.ident[:, :]).then_inc(S["turned"], 1)
                    j = t - 1
                    if hidden and 0 <= j < UB:
                        pe.wait_ge(S["col"], i * UB + j + 1)
                        if j >= 2:
                            pe.wait_ge(S["hid"], i * UB + j - 1)
                        nc.tensor.matmul(m.ps[:, 2 + j % 2, 0:P], hidden[0][:, :], col[:, j, :], start=True, stop=True).then_inc(S["hid_psum"], 1)
                    j = t - 2
                    if j >= 0:
                        pe.wait_ge(S["hid"] if hidden else S["col"], i * UB + j + 1)
                        free(pe, S["emptied"], i, j)
                        nc.tensor.matmul(m.ps[:, 4 + j % 2, 0:width], (hid if hidden else col)[:, j, :], rhs, start=True, stop=True).then_inc(S["out"], 1)

        @block.vector
        def _(v):
            step = chain(v, S["dve"])
            before(v, step)
            v.sem_inc(S["rows_ok"], 1)
            with v.Fori(0, NB // UB) as i:
                for j in range(UB):
                    v.wait_ge(S["out"], i * UB + j + 1 + UB)
                    use(v, i * UB + j, m.ps[:, 4 + j % 2, 0:width]).then_inc(S["emptied"], 1)
            v.wait_ge(S["emptied"], NB + 2)
            after(v, step)


def layernorm(nc, m, name, store, before=None, after=None):
    sq = m.gather[:, 0:NB * D].rearrange("p (b d) -> p b d", d=D)
    halves = (slice(0, NB // 2), slice(NB // 2, NB))
    with phase(nc, name, "dve centered squared var root done stored") as (S, block):
        @block.vector
        def _(v):
            V, step = nc.vector, chain(v, S["dve"])
            if before:
                before(v, step)
            mean, rstd = m.mv[:, :, 0], m.rstd
            step(V.tensor_reduce(mean, m.x[:, :, :], AX.X, ALU.add))
            step(V.tensor_scalar(mean, mean, 1.0 / D, None, ALU.mult))
            for h in halves:
                V.tensor_tensor(m.x[:, h, :], m.x[:, h, :], bcast(mean[:, h]), ALU.subtract).then_inc(S["centered"], 1)
            for k, h in enumerate(halves):
                v.wait_ge(S["squared"], k + 1)
                step(V.tensor_reduce(rstd[:, h], sq[:, h, :], AX.X, ALU.add))
            V.tensor_scalar(rstd[:, :], rstd[:, :], 1.0 / D, 1e-5, ALU.mult, ALU.add).then_inc(S["var"], 1)
            v.wait_ge(S["root"], 1)
            step(V.reciprocal(rstd[:, :], rstd[:, :]))
            v.wait_ge(S["centered"], 2)
            step(V.tensor_tensor(m.x[:, :, :], m.x[:, :, :], bcast(rstd[:, :]), ALU.mult))
            if after:
                after(v, step)
            v.sem_inc(S["done"], 1)

        @block.scalar
        def _(act):
            for k, h in enumerate(halves):
                act.wait_ge(S["centered"], k + 1)
                nc.scalar.activation(sq[:, h, :], m.x[:, h, :], ACT.Square).then_inc(S["squared"], 1)
            act.wait_ge(S["var"], 1)
            nc.scalar.activation(m.rstd[:, :], m.rstd[:, :], ACT.Sqrt).then_inc(S["root"], 1)

        if store:
            @block.sync
            def _(sp):
                sp.wait_ge(S["done"], 1)
                for dst, src in store:
                    sp.dma_start(dst, src).then_inc(S["stored"], 16)
                sp.wait_ge(S["stored"], 16 * len(store))


def windows_of_buckets(nc, m):
    with phase(nc, "windows", "dve cmp in_psum") as (S, block):
        @block.vector
        def _(v):
            V, step = nc.vector, chain(v, S["dve"])
            V.tensor_scalar(m.tabs[0:NB, :], m.tF[0:NB, :], m.endp[0:NB, 0:1], None, ALU.is_ge).then_inc(S["cmp"], 1)
            v.wait_ge(S["in_psum"], 2)
            for k in range(2):
                step(V.tensor_scalar(m.start[:, k * (BT // 2):(k + 1) * (BT // 2)], m.ps[:, k, 0:BT // 2], float(P), None, ALU.mult))
            step(V.tensor_copy(m.startI[0:1, :], m.start[0:1, :]))
            step(V.memset(m.dst[:, :], 0.0))
            step(V.memset(m.off[:, :], -1.0))

        @block.tensor
        def _(pe):
            pe.wait_ge(S["cmp"], 1)
            for k in range(2):
                nc.tensor.matmul(m.ps[:, k, 0:BT // 2], m.ones[0:NB, :], m.tabs[0:NB, k * (BT // 2):(k + 1) * (BT // 2)],
                                 start=True, stop=True).then_inc(S["in_psum"], 1)


def attend(nc, m, a):
    J = U3 // G
    C = U3 // Q3
    IT = BT // U3
    W2 = 2 * D
    g = m.gather[:, 0:U3 * W2].rearrange("p (t d) -> p t d", d=W2)
    attr = m.erow[:, :, :].rearrange("p t d -> p (t d)")[:, 0:U * DE].rearrange("p (t d) -> p t d", d=DE)
    with phase(nc, "attend", f"rows*{RG} landed*{J} idx_ready used now turned copied onehot hidden summed scored "
                             "max_in max_turned max_new max_spread max_set negated expd z weights added masked fell distance reset") as (S, block):
        def reached(eng, sem, value):
            if not (isinstance(value, int) and value <= 0):
                eng.wait_ge(sem, value)

        def run(eng, body, behind):
            body(0, range(J), lambda r: r >= 0)
            with eng.Fori(1, IT) as i:
                body(i, range(J), lambda r: True)
            if behind:
                body(IT - 1, range(J, J + behind), lambda r: r < J)

        def snap(eng, x):
            return x if isinstance(x, int) else eng.snap(x)

        @block.sync
        def _(sp):
            def body(i, slots, exists):
                n0 = snap(sp, i * J)
                for s in slots:
                    if not (isinstance(i, int) and s < RG):
                        hold(sp, S["turned"], n0 + (s - RG + 1))
                    k = s % RG * G
                    sp.dma_start(attr[:, k:k + G, :],
                                 a.bucketed[bass.ds((i * U3 + s * G) * P, G * P), 0:DE].rearrange("(t p) d -> p t d", p=P)).then_inc(S["rows"][s % RG], 16)
            run(sp, body, 0)

        @block.gpsimd
        def _(pool):
            def body(i, slots, exists):
                n0 = snap(pool, i * J)
                for s in slots:
                    hold(pool, S["idx_ready"], n0 + (s + 1))
                    if not isinstance(i, int):
                        hold(pool, S["used"], n0 + (s - J + 1))
                    for k in range(G * s, G * s + G):
                        nc.gpsimd.indirect_dma_start(g[:, k, :], None, a.table2,
                                                     bass.IndirectOffsetOnAxis(m.idx[:, k:k + 1], 0)).then_inc(S["landed"][s], 16)
            run(pool, body, 0)

        @block.scalar
        def _(act):
            A = nc.scalar

            def cast(j, tile):
                A.copy(m.idx[:, j * G:(j + 1) * G], m.dst[:, bass.ds(tile, G)]).then_inc(S["idx_ready"], 1)
            for j in range(J):
                cast(j, j * G)

            def body(i, slots, exists):
                n0, q0 = snap(act, i * J), snap(act, i * C)
                t0 = snap(act, i * U3)
                for s in slots:
                    if exists(s):
                        reached(act, S["weights"], n0 + (s - J + 1))
                        A.copy(m.now[:, s * G:(s + 1) * G], m.off[:, bass.ds(t0 + s * G, G)]).then_inc(S["now"], 1)
                        if not (isinstance(i, int) and s < J - 4):
                            act.wait_ge(S["summed"], n0 + (s + 4 - J + 1))
                            cast((s + 4) % J, t0 + (s + 4) * G)
                        h = s % 2
                        act.wait_ge(S["now"], n0 + (s + 1))
                        reached(act, S["onehot"], n0 + s)
                        for e in range(G):
                            last = A.activation(m.junk[:, e, :], m.iota[:, :], ACT.Square, scale=-1.0, bias=m.now[:, s * G + e:s * G + e + 1])
                        last.then_inc(S["distance"], 1)
                        act.wait_ge(S["distance"], n0 + (s + 1))
                        reached(act, S["turned"], n0 + (s - 2 + 1))
                        A.activation(m.ohb[:, G * h:G * h + G, :], m.junk[:, 0:G, :], ACT.Relu, scale=-1.0, bias=m.ones[:, 0:1]).then_inc(S["onehot"], 1)
                    r = s - 2
                    if exists(r):
                        h = r % 2
                        act.wait_ge(S["turned"], n0 + (r + 1))
                        reached(act, S["hidden"], n0 + (r - 2 + 1))
                        A.copy(m.eT[:, 2 * h:2 * h + 2, :], m.ps[:, h, 0:2 * P].rearrange("p (t e) -> p t e", t=2)).then_inc(S["copied"], 1)
                        A.copy(m.ohT[:, G * h:G * h + G, :], m.psb[:, h, 4 * P:8 * P].rearrange("p (t e) -> p t e", t=G)).then_inc(S["copied"], 1)
                    r = s - 5
                    if s % 2 and exists(r):
                        q = r // 2
                        act.wait_ge(S["negated"], q0 + (q + 1))
                        k = q % C
                        A.activation(m.c[:, k:k + 1], m.dif[:, 0:1], ACT.Exp).then_inc(S["expd"], 1)
                        A.activation(m.p[:, k * Q3:(k + 1) * Q3], m.sc[:, k * Q3:(k + 1) * Q3], ACT.Exp, bias=m.negm[:, 0:1],
                                     accum_out=m.zq[:, k % 2:k % 2 + 1]).then_inc(S["expd"], 1)
            run(act, body, 4)

        @block.tensor
        def _(pe):
            T = nc.tensor

            def body(i, slots, exists):
                n0, q0 = snap(pe, i * J), snap(pe, i * C)
                t0, c0, a0, r0 = snap(pe, i * U3), snap(pe, i * 2 * J), snap(pe, i * G * J), snap(pe, i * (J // RG) * 16)
                for s in slots:
                    if exists(s):
                        h = s % 2
                        hold(pe, S["rows"][s % RG], r0 + (s // RG + 1) * 16)
                        pe.wait_ge(S["onehot"], n0 + (s + 1))
                        if not (isinstance(i, int) and s < 2):
                            hold(pe, S["copied"], c0 + 2 * (s - 2 + 1))
                        k = s % RG * G
                        for e in range(2):
                            T.transpose(m.ps[:, h, e * P:(e + 1) * P], attr[:, k + 2 * e:k + 2 * e + 2, :].rearrange("p t d -> p (t d)"), m.ident[:, :])
                        for e in range(G):
                            last = T.transpose(m.psb[:, h, (4 + e) * P:(5 + e) * P], m.ohb[:, G * h + e, :], m.identb[:, :])
                        last.then_inc(S["turned"], 1)
                    q = (s - 3) // 2
                    if s % 2 and exists(s - 3):
                        pe.wait_ge(S["max_in"], q0 + (q + 1))
                        T.transpose(m.ps[0:1, 6, 0:P], m.mx[:, 0:1], m.ident[:, :]).then_inc(S["max_turned"], 1)
                    r = s - 1
                    if exists(r):
                        h = r % 2
                        start = window_starts(nc, mybir.EngineType.PE, m, t0 + r * G, G)
                        pe.wait_ge(S["copied"], c0 + 2 * (r + 1))
                        reached(pe, S["summed"], n0 + (r - 2 + 1))
                        for e in range(G):
                            out = m.ps[:, 2 + h, e * P:(e + 1) * P]
                            T.matmul(out, m.eT[:, 2 * h + e // 2, :], m.Wh[:, e % 2, :], start=True, stop=False)
                            last = T.matmul(out, m.ohT[:, G * h + e, :], m.side[:, bass.ds(start[e], P)], start=False, stop=True)
                        last.then_inc(S["hidden"], 1)
                    if s % 2 and exists(s - 3):
                        pe.wait_ge(S["max_new"], q0 + (q + 1))
                        T.matmul(m.ps[:, 7, 0:1], m.ones[0:1, :], m.mnew[0:1, 0:1], start=True, stop=True).then_inc(S["max_spread"], 1)
                    r = s - 4
                    if exists(r):
                        h = r % 2
                        pe.wait_ge(S["weights"], n0 + (r + 1))
                        reached(pe, S["added"], a0 + G * (r - 2 + 1))
                        for e in range(G):
                            last = T.matmul(m.ps[:, 4 + h, e * P:(e + 1) * P], g[:, r % J * G + e, 0:D], m.oh[:, G * h + e, :], start=True, stop=True)
                        last.then_inc(S["used"], 1)
            run(pe, body, 4)

        @block.vector
        def _(v):
            V, step = nc.vector, chain(v, S["reset"])
            step(V.memset(m.mrep[:, :], LOW))
            step(V.memset(m.hist[:, :], LOW))
            step(V.memset(m.z[:, :], 0.0))

            def body(i, slots, exists):
                n0, q0, q2 = snap(v, i * J), snap(v, i * C), snap(v, i * 2 * C)
                t0, a0, l0 = snap(v, i * U3), snap(v, i * G * J), snap(v, i * 16 * G)
                for s in slots:
                    q = (s - 4) // 2
                    if s % 2 == 0 and exists(s - 4):
                        v.wait_ge(S["max_turned"], q0 + (q + 1))
                        V.tensor_reduce(m.mnew[0:1, 1:2], m.ps[0:1, 6, 0:P], AX.X, ALU.max).then_inc(S["max_set"], 1)
                        v.wait_ge(S["max_set"], q2 + (2 * q + 1))
                        V.tensor_tensor(m.mnew[0:1, 0:1], m.mnew[0:1, 1:2], m.mrep[0:1, 0:1], ALU.max).then_inc(S["max_new"], 1)
                    r = s - 5
                    if exists(r):
                        h, q5 = r % 2, r // 2
                        v.wait_ge(S["expd"], q2 + 2 * (q5 + 1))
                        if r % 2 == 0:
                            reached(v, S["z"], q0 + q5)
                            k = q5 % C
                            V.tensor_scalar(m.z[:, 0:1], m.z[:, 0:1], m.c[:, k:k + 1], m.zq[:, k % 2:k % 2 + 1], ALU.mult, ALU.add).then_inc(S["z"], 1)
                        reached(v, S["used"], n0 + (r - 2 + 1))
                        for e in range(G):
                            k = r % J * G + e
                            last = V.tensor_scalar(m.oh[:, G * h + e, :], m.iota[:, :], m.now[:, k:k + 1], m.p[:, k:k + 1], ALU.is_equal, ALU.mult)
                        last.then_inc(S["weights"], 1)
                    r6 = s - 6
                    if exists(r6):
                        start = window_starts(nc, mybir.EngineType.DVE, m, t0 + r6 * G, G)
                        v.wait_ge(S["used"], n0 + (r6 + 1))

                    def add(e):
                        if exists(r6):
                            reached(v, S["added"], a0 + (r6 * G + e))
                            w, ps = m.agg[:, bass.ds(start[e], WIN)], m.ps[:, 4 + r6 % 2, e * P:(e + 1) * P]
                            if r6 % 2 == 0 and e == 0:
                                k = r6 // 2 % C
                                V.scalar_tensor_tensor(w, w, m.c[:, k:k + 1], ps, ALU.mult, ALU.add).then_inc(S["added"], 1)
                            else:
                                V.tensor_tensor(w, w, ps, ALU.add).then_inc(S["added"], 1)
                    add(0)
                    add(1)
                    r = s - 2
                    if exists(r):
                        h = r % 2
                        v.wait_ge(S["hidden"], n0 + (r + 1))
                        v.wait_ge(S["landed"][r % J], l0 + (r // J + 1) * 16 * G)
                        reached(v, S["scored"], n0 + (r - 2 + 1))
                        k = r % J * G
                        V.tensor_tensor(m.hid[:, G * h:G * h + G, :], m.ps[:, 2 + h, 0:G * P].rearrange("p (t d) -> p t d", t=G),
                                        g[:, k:k + G, D:W2], ALU.add).then_inc(S["summed"], 1)
                    if s % 2 == 0 and exists(s - 4):
                        v.wait_ge(S["max_spread"], q0 + (q + 1))
                        reached(v, S["expd"], q2 + 2 * q)
                        V.tensor_tensor(m.dif[:, 0:1], m.mrep[:, 0:1], m.ps[:, 7, 0:1], ALU.subtract).then_inc(S["fell"], 1)
                        V.tensor_copy(m.hist[:, bass.ds(q0 + q, 1)], m.ps[:, 7, 0:1])
                        V.tensor_scalar(m.negm[:, 0:1], m.ps[:, 7, 0:1], -1.0, None, ALU.mult).then_inc(S["negated"], 1)
                        v.wait_ge(S["fell"], q0 + (q + 1))
                        V.tensor_copy(m.mrep[:, 0:1], m.ps[:, 7, 0:1]).then_inc(S["max_set"], 1)
                    q = (s - 3) // 2
                    if s % 2 and exists(s - 3):
                        k = q % C
                        v.wait_ge(S["now"], n0 + (s - 2 + 1))
                        V.tensor_scalar(m.valid[:, 0:Q3], m.now[:, k * Q3:(k + 1) * Q3], 0.0, LOW, ALU.is_lt, ALU.mult).then_inc(S["masked"], 1)
                    add(2)
                    if exists(r):
                        v.wait_ge(S["summed"], n0 + (r + 1))
                        for e in range(G):
                            k = r % J * G + e
                            last = V.scalar_tensor_tensor(m.hid[:, G * h + e, :], m.hid[:, G * h + e, :], 0.0, m.bias[:, 5, :], ALU.max, ALU.mult,
                                                          accum_out=m.sc[:, k:k + 1])
                        last.then_inc(S["scored"], 1)
                    add(3)
                    if s % 2 and exists(s - 3):
                        cols = slice(q % C * Q3, (q % C + 1) * Q3)
                        v.wait_ge(S["scored"], n0 + (s - 2 + 1))
                        v.wait_ge(S["masked"], q2 + (2 * q + 1))
                        V.tensor_tensor(m.sc[:, cols], m.sc[:, cols], m.valid[:, 0:Q3], ALU.add).then_inc(S["masked"], 1)
                        v.wait_ge(S["masked"], q2 + (2 * q + 2))
                        V.tensor_reduce(m.mx[:, :], m.sc[:, cols], AX.X, ALU.max).then_inc(S["max_in"], 1)
            run(v, body, 6)


def gnn_kernel(nc, x, src, dst, attr, ew, w1, b1, w2, b2, hw, W, b, Wh, bh, Wn, bn, we, ft, ftb, out):
    with ExitStack() as ctx, nc.allow_non_contiguous_dma(reason="2400 hyperedge weights"):
        def sb(name, shape, dt=FP32):
            return ctx.enter_context(nc.sbuf_tensor(name, shape, dt))

        a = Names()
        a.x, a.src, a.dst, a.attr, a.ew, a.hw = x, src, dst, attr, ew, hw
        a.w1, a.b1, a.w2, a.b2, a.W, a.b = w1, b1, w2, b2, W, b
        a.Wh, a.bh, a.Wn, a.bn, a.we, a.ft, a.ftb = Wh, bh, Wn, bn, we, ft, ftb
        a.table = nc.dram_tensor("node_table", (NP, D), FP32).ap()
        a.table2 = nc.dram_tensor("node_table_xq", (NP, 2 * D), FP32).ap()
        a.bucketed = nc.dram_tensor("bucketed_edges", (BT * P, ROW), FP32).ap()
        m = Names()
        m.x, m.t = sb("x_nodes", [P, NB, D]), sb("t_nodes", [P, NB, D])
        m.agg, m.side = sb("agg", [P, AW]), sb("side_rows", [P, AW])
        m.gather = sb("gathered", [P, U3 * 2 * D])
        up = m.gather[:, U * D:]
        m.scratch = up
        m.wide = up[:, 0:NT].bitcast(I32)
        m.dhi, m.dlo, m.cum = up[:, NT:2 * NT], up[:, 2 * NT:3 * NT], up[:, 3 * NT:4 * NT]
        m.shi, m.slo = up[:, 5 * CH * P:5 * CH * P + NT], up[:, 5 * CH * P + NT:5 * CH * P + 2 * NT]
        m.cumhi = up[:, 0:U * NB].rearrange("p (t b) -> p t b", b=NB)
        low = m.gather[:, 0:U * D].bitcast(BF16)
        m.ohlo = low[:, 0:U * P].rearrange("p (t n) -> p t n", n=P)
        m.ohhi = low[:, U * P:U * P + U * NB].rearrange("p (t n) -> p t n", n=NB)
        m.erow = sb("edge_rows", [P, U, ROW])
        BX = BT + U3
        m.src, m.dst, m.ew = sb("src_t", [P, NT]), sb("dst_t", [P, BX]), sb("ew_t", [P, BT])
        m.off, m.start, m.rank = sb("off_t", [P, BT]), sb("start_t", [P, BT]), sb("rank_t", [P, NT])
        m.hwe = sb("hwe_t", [P, NT])
        m.tabs = sb("tabs", [P, BT])
        m.tI = sb("tile_iota_i", [P, BT], I32)
        m.tF = m.tI[:, :].bitcast(FP32)
        m.startI = sb("start_i", [1, BT], I32)
        m.idx = sb("idx", [P, U3], I32)
        m.clampf = sb("clampf", [P, U])
        m.oh = sb("onehots", [P, 8, P])
        m.junk = sb("junk", [P, 4, P])
        m.picked = sb("picked", [P, U])
        m.iotaI, m.pidxI = sb("iota_i", [P, P], I32), sb("pidx_i", [P, 1], I32)
        m.iota, m.iotab, m.pidx = sb("iota", [P, P]), sb("iota_b", [P, P], BF16), sb("pidx", [P, 1])
        m.ident, m.identb, m.tri, m.ones = sb("ident", [P, P]), sb("ident_b", [P, P], BF16), sb("tri", [P, P]), sb("ones", [P, P])
        m.zerob, m.zerof = sb("zero_b", [P, P], BF16), sb("zero_f", [P, P])
        m.w1, m.w2, m.W = sb("w1", [P, D]), sb("w2", [P, D]), sb("W", [P, D])
        m.w1T, m.w2T, m.WT = sb("w1T", [P, D]), sb("w2T", [P, D]), sb("WT", [P, D])
        m.Wh, m.Wn, m.ft = sb("Wh", [P, 2, D]), sb("Wn", [P, 2, D]), sb("ft", [P, D])
        m.bias, m.b1 = sb("biases", [P, 6, D]), sb("b1", [P, 1])
        m.hwn = sb("hw_nodes", [P, MB])
        nb = lambda n, dt=FP32: sb(n, [P, NB], dt)
        m.dinv, m.deg, m.de, m.dv, m.cnt, m.first, m.ends, m.bF, m.rstd, m.fac = (
            nb(n) for n in ("dinv", "deg", "de", "dv", "cnt", "first", "ends", "bF", "rstd", "fac"))
        m.bI = nb("bI", I32)
        m.endp = sb("endp", [P, 1])
        m.tmin, m.tmax, m.span, m.shift = sb("tmin", [P, CH]), sb("tmax", [P, CH]), sb("span", [P, 1]), sb("shift", [P, 1])
        m.small, m.smallI, m.lasthe = sb("small", [P, 8]), sb("smallI", [1, 8], I32), sb("lasthe", [P, 1])
        m.mv7, m.stats, m.mv = sb("mv7", [P, UB, 2]), sb("stats", [P, UB, 6]), sb("mv", [P, NB, 2])
        m.eT, m.ohT, m.ohb = sb("eT", [P, 4, P]), sb("ohT", [P, 2 * G, P]), sb("ohb", [P, 2 * G, P], BF16)
        m.hid, m.now = sb("hid", [P, 2 * G, D]), sb("off_now", [P, U3])
        m.wnow = sb("weight_now", [P, U])
        m.sc, m.p = sb("scores", [P, U3]), sb("probs", [P, U3])
        m.mrep, m.mx, m.mnew, m.dif, m.negm, m.zq, m.z = (sb(n, [P, 2]) for n in ("mrep", "mx2", "mnew", "dif", "negm", "zq", "z"))
        m.mx = m.mx[:, 0:1]
        m.c = sb("c", [P, U3 // Q3])
        m.valid = sb("valid", [P, 2 * Q3])
        m.hist = sb("max_hist", [P, BT // Q3])
        m.ps = ctx.enter_context(nc.psum_tensor("ps", [P, 8, 512], FP32))
        m.psb = m.ps[:, :, :].bitcast(BF16)
        V = nc.vector
        blk = lambda t, i: t[:, bass.ds(i, 1), :].rearrange("p o d -> p (o d)")
        prepare(nc, m, a)

        edges = dict(table=a.table, dst_order=True)
        aggregate(nc, m, a, "hop1", idx=m.src, iters=NI, side=HyperedgeWeights(nc, m), **edges)
        bucket_starts(nc, m)

        def add_self(v, i, ps):
            return V.tensor_tensor(blk(m.t, i), blk(m.t, i), ps, ALU.add)

        def hop1(v, step):
            t, x = m.t[:, :, :], m.x[:, :, :]
            step(V.tensor_tensor(t, t, bcast(m.dinv[:, :]), ALU.mult))
            step(V.tensor_tensor(t, t, x, ALU.add))
            step(V.tensor_scalar(m.bF[:, :], m.dinv[:, :], 0.5, None, ALU.mult))
            step(V.tensor_tensor(t, t, bcast(m.bF[:, :]), ALU.mult))
        agg_blocks(nc, m, "hop1_out", NB, UB, None, add_self, hop1, [(node_view(a.table, NP), m.t[:, :, :])])
        aggregate(nc, m, a, "hop2", idx=m.src, iters=NI, side=BucketRanks(nc, m), **edges)
        bucket_edges(nc, m, a)

        def hop2(v, step):
            t, x = m.t[:, :, :], m.x[:, :, :]
            step(V.tensor_tensor(t, t, bcast(m.dinv[:, :]), ALU.mult))
            step(V.tensor_tensor(t, t, x, ALU.add))
            step(V.tensor_scalar(t, t, 0.5, 0.0, ALU.mult, ALU.max))
        agg_blocks(nc, m, "hop2_out", NB, UB, None, add_self, hop2, None)
        row_blocks(nc, m, "mlp", m.t, m.w2T[:, :], D,
                   use=lambda v, i, ps: V.tensor_tensor(blk(m.x, i), blk(m.x, i), ps, ALU.add),
                   before=lambda v, step: None,
                   after=lambda v, step: step(V.tensor_tensor(m.x[:, :, :], m.x[:, :, :],
                                              m.bias[:, 0:1, :].to_broadcast([P, NB, D]), ALU.add)),
                   hidden=(m.w1T, m.b1))

        def scale_dv(v, step):
            step(V.tensor_tensor(m.t[:, :, :], m.x[:, :, :], bcast(m.dv[:, :]), ALU.mult))
        layernorm(nc, m, "norm0", [(node_view(a.table, NP), m.t[:, :, :])], after=scale_dv)
        aggregate(nc, m, a, "hyperedges", idx=m.src, iters=m.smallI[0:1, 1:2], **edges)

        def he_weight(v, step):
            n = (MB, 1)
            step(V.reciprocal(m.bF[:, 0:MB], m.de[:, 0:MB]))
            step(V.tensor_tensor(m.bF[:, 0:MB], m.bF[:, 0:MB], m.hwn[:, :], ALU.mult))
            step(V.tensor_tensor(m.t[:, 0:MB, :], m.t[:, 0:MB, :], bcast(m.bF[:, 0:MB]), ALU.mult))
        agg_blocks(nc, m, "he_out", MB, 5, None, lambda v, i, ps: V.tensor_copy(blk(m.t, i), ps), he_weight,
                   [(node_view(a.table, MB * P), m.t[:, 0:MB, :])])
        windows_of_buckets(nc, m)
        groups = m.smallI[0:1, 2:3]
        aggregate(nc, m, a, "members", table=a.table, idx=m.dst, dst_order=False, iters=groups, last_he=True, load_rows=True)

        def add_bias(v, step):
            step(V.tensor_tensor(m.x[:, :, :], m.x[:, :, :], m.bias[:, 1:2, :].to_broadcast([P, NB, D]), ALU.add))
        agg_blocks(nc, m, "members_out", NB, UB, m.WT,
                   lambda v, i, ps: V.scalar_tensor_tensor(blk(m.x, i), ps, m.dv[:, bass.ds(i, 1)], blk(m.x, i), ALU.mult, ALU.add),
                   add_bias, None)
        layernorm(nc, m, "norm1", [(node_view(a.table, NP), m.x[:, :, :])])

        aggregate(nc, m, a, "light", table=a.table, idx=m.dst, dst_order=False, iters=groups, weight=m.ew)
        agg_blocks(nc, m, "light_out", NB, UB, None,
                   lambda v, i, ps: V.scalar_tensor_tensor(blk(m.t, i), ps, 3.0, blk(m.x, i), ALU.mult, ALU.add),
                   lambda v, step: step(V.scalar_tensor_tensor(m.x[:, :, :].rearrange("p b d -> p (b d)"),
                                        m.t[:, :, :].rearrange("p b d -> p (b d)"), 0.25,
                                        m.x[:, :, :].rearrange("p b d -> p (b d)"), ALU.mult, ALU.add)), None)
        layernorm(nc, m, "norm2", [(node_view(a.table2[:, 0:D], NP), m.x[:, :, :])])

        def pq(v, i, ps):
            V.tensor_copy(m.side[:, bass.ds(i * P, P)], ps[:, 0:D])
            return V.tensor_copy(blk(m.t, i), ps[:, D:2 * D])

        def pq_bias(v, step):
            pn = m.side[:, 0:NP].rearrange("p (b d) -> p b d", d=D)
            for k in (2, 3):
                step(V.tensor_tensor(pn, pn, m.bias[:, k:k + 1, :].to_broadcast([P, NB, D]), ALU.add))
        row_blocks(nc, m, "pq", m.x, m.Wn[:, :, :].rearrange("p k d -> p (k d)"), 2 * D, pq, lambda v, step: None, pq_bias)
        store_q(nc, m, a)
        attend(nc, m, a)
        softmax_factors(nc, m)
        agg_blocks(nc, m, "attend_out", NB, UB, None,
                   lambda v, i, ps: V.scalar_tensor_tensor(blk(m.t, i), ps, m.fac[:, bass.ds(i, 1)], blk(m.x, i), ALU.mult, ALU.add),
                   lambda v, step: None, None, clear=False)

        def last(v, step):
            step(V.tensor_tensor(m.x[:, :, :], m.x[:, :, :], m.t[:, :, :], ALU.add))
            step(V.tensor_tensor(m.x[:, :, :], m.x[:, :, :], m.bias[:, 4:5, :].to_broadcast([P, NB, D]), ALU.add))
        row_blocks(nc, m, "ft", m.t, m.ft[:, :], D,
                   lambda v, i, ps: V.tensor_tensor(blk(m.x, i), blk(m.x, i), ps, ALU.add), lambda v, step: None, last)
        layernorm(nc, m, "norm3", [(node_view(out, (NB - 1) * P), m.x[:, 0:NB - 1, :]), (out[(NB - 1) * P:N, :], m.x[0:NH, NB - 1, :])])


def store_q(nc, m, a):
    with phase(nc, "store_q", "stored") as (S, block):
        @block.sync
        def _(sp):
            sp.dma_start(node_view(a.table2[:, D:2 * D], NP), m.t[:, :, :]).then_inc(S["stored"], 16)
            sp.wait_ge(S["stored"], 16)


def softmax_factors(nc, m):
    NQ = BT // Q3
    with phase(nc, "factors", "dve z_in_psum dif expd diag fac_psum") as (S, block):
        @block.vector
        def _(v):
            V, step = nc.vector, chain(v, S["dve"])
            mask = m.tabs[0:NB, 0:NQ]
            h = m.tabs[0:NB, NQ:2 * NQ]
            step(V.tensor_scalar(mask, m.tF[0:NB, 0:NQ], float(Q3), m.endp[0:NB, 0:1], ALU.mult, ALU.is_lt))
            step(V.tensor_tensor(h, m.hist[0:NB, :], mask, ALU.mult))
            step(V.tensor_scalar(mask, mask, -1.0, -LOW, ALU.add, ALU.mult))
            step(V.tensor_tensor(h, h, mask, ALU.add))
            step(V.tensor_reduce(m.small[0:NB, 5:6], h, AX.X, ALU.max))
            V.tensor_tensor(m.small[0:NB, 5:6], m.small[0:NB, 5:6], m.mrep[0:NB, 0:1], ALU.subtract).then_inc(S["dif"], 1)
            v.wait_ge(S["expd"], 1)
            V.tensor_scalar(m.oh[0:NB, 0, 0:NB], m.ident[0:NB, 0:NB], m.small[0:NB, 6:7], None, ALU.mult).then_inc(S["diag"], 1)
            v.wait_ge(S["z_in_psum"], 1)
            step(V.reciprocal(m.small[:, 7:8], m.ps[:, 0, 0:1]))
            v.wait_ge(S["fac_psum"], 1)
            step(V.tensor_scalar(m.fac[:, :], m.ps[:, 1, 0:NB], m.small[:, 7:8], -1.0, ALU.mult, ALU.mult))

        @block.scalar
        def _(act):
            act.wait_ge(S["dif"], 1)
            nc.scalar.activation(m.small[0:NB, 6:7], m.small[0:NB, 5:6], ACT.Exp).then_inc(S["expd"], 1)

        @block.tensor
        def _(pe):
            nc.tensor.matmul(m.ps[:, 0, 0:1], m.ones[:, :], m.z[:, 0:1], start=True, stop=True).then_inc(S["z_in_psum"], 1)
            pe.wait_ge(S["diag"], 1)
            nc.tensor.matmul(m.ps[:, 1, 0:NB], m.ones[0:NB, :], m.oh[0:NB, 0, 0:NB], start=True, stop=True).then_inc(S["fac_psum"], 1)


_INS = ["x", "src", "dst", "edge_attr_64", "edge_weight", "L0_gnn_w1", "L0_gnn_b1", "L0_gnn_w2", "L0_gnn_b2",
        "L1_gnn_hyperedge_weight", "L1_gnn_W", "L1_gnn_b", "L3_gnn_Wh_w", "L3_gnn_Wh_b", "L3_gnn_Wn_w", "L3_gnn_Wn_b",
        "L3_gnn_w_e", "L3_gnn_ft_w", "L3_gnn_ft_b"]


def kernel(**inputs):
    import numpy as _np
    import concourse.bacc as _bacc
    from concourse import mybir as _mybir
    from concourse.bass_utils import run_bass_kernel_spmd as _run

    nc = _bacc.Bacc("TRN2", target_bir_lowering=False, num_devices=1)
    nc.disable_value_cache = True
    arrays, args = {}, []
    for name in _INS:
        a = _np.ascontiguousarray(inputs[name])
        arrays[f"in_{name}_dram"] = a
        args.append(nc.dram_tensor(f"in_{name}_dram", a.shape, _mybir.dt.from_np(a.dtype), kind="ExternalInput").ap())
    args.append(nc.dram_tensor("out_0_dram", (N, D), _mybir.dt.float32, kind="ExternalOutput").ap())
    gnn_kernel(nc, *args)
    r = _run(nc, [arrays], core_ids=[0])
    return r.results[0]["out_0_dram"]
```
